# Optimizing a Trainium2 kernel written in Bass

```python
import numpy as np
import jax
import jax.numpy as jnp

def _softmax(x, axis=-1):
    return jax.nn.softmax(x, axis=axis)

def _gelu(x):
    return jax.nn.gelu(x, approximate=True)

def _silu(x):
    return jax.nn.silu(x)

def _sigmoid(x):
    return jax.nn.sigmoid(x)

def _layernorm(x, axis=-1, eps=1e-05):
    m = jnp.mean(x, axis=axis, keepdims=True)
    v = jnp.var(x, axis=axis, keepdims=True)
    return (x - m) / jnp.sqrt(v + eps)

def _scatter_add(tgt, idx, src, axis=0):
    return tgt.at[idx].add(src)

def _segment_sum(src, seg, n):
    return jax.ops.segment_sum(src, seg, n)
kernel_name = 'mk_decoder_postln_d1_seqx_r8_88a288'

def setup_inputs(seed: int=0):
    np.random.seed(seed)
    _w = jnp.asarray

    def _rec_inputs():
        import jax
        import jax.numpy as jnp
        _rk = jax.random.key(seed)
        x = -0.0002928 + 1 * jax.random.normal(jax.random.fold_in(_rk, 1), (32, 64, 128), jnp.float32)
        _lenS = 64 - jax.random.randint(jax.random.fold_in(_rk, 7), (32,), 0, max(1, 64 // 4) + 1, jnp.int32)
        _lenS2 = 64 - jax.random.randint(jax.random.fold_in(_rk, 8), (32,), 0, max(1, 64 // 4) + 1, jnp.int32)
        _ctx_1024P = jax.random.normal(jax.random.fold_in(_rk, 11), (32, 16, 128), jnp.float32)
        _ctx_1024c = jax.random.dirichlet(jax.random.fold_in(_rk, 511), 0.3 * jnp.ones((16,), jnp.float32), (32, 64))
        _ctx_1024t = jnp.einsum('bsk,bkd->bsd', _ctx_1024c, _ctx_1024P)
        _ctx_1024t = _ctx_1024t * jax.lax.rsqrt(jnp.mean(jnp.square(_ctx_1024t)) + 1e-12) * 0.953939
        ctx_1024 = -1.39393e-06 + 0.999914 * (_ctx_1024t + 0.3 * jax.random.normal(jax.random.fold_in(_rk, 611), (32, 64, 128), jnp.float32))
        _validS = jnp.arange(64)[None, :] < _lenS[:, None]
        _validS2 = jnp.arange(64)[None, :] < _lenS2[:, None]
        _causal = jnp.tril(jnp.ones((64, 64), dtype=bool))
        mask_BxS2_fk1 = jnp.where(jnp.broadcast_to(_validS2[:, :], (32, 64)), 1.0, 0.0).astype(jnp.float32)
        return (x, ctx_1024, mask_BxS2_fk1)
    x, ctx_1024, mask_BxS2_fk1 = _rec_inputs()

    def _L0_attn_setup():
        import jax, jax.numpy as jnp
        import numpy as np
        D_MODEL = 128
        N_HEADS = 16
        D_HEAD = 64
        D_REC = N_HEADS * D_HEAD
        BATCH = 4
        SEQ = 1024
        CHUNK = 64

        def _make_decay_bias():
            n_fast, n_medium, n_slow = (5, 6, 5)
            b = np.zeros(D_REC, dtype=np.float32)
            fast_end = n_fast * D_HEAD
            medium_end = (n_fast + n_medium) * D_HEAD
            b[:fast_end] = -2.2
            b[fast_end:medium_end] = 0.0
            b[medium_end:] = 4.6
            return jnp.asarray(b)

        def _chunked_scan(decay, value, chunk_size=CHUNK):
            b, s, d = decay.shape
            pad = -s % chunk_size
            if pad:
                decay = jnp.pad(decay, ((0, 0), (0, pad), (0, 0)), constant_values=1.0)
                value = jnp.pad(value, ((0, 0), (0, pad), (0, 0)))
            total = s + pad
            n = total // chunk_size
            dc = decay.reshape(b, n, chunk_size, d)
            vc = value.reshape(b, n, chunk_size, d)
            cum_log = jnp.cumsum(jnp.log(jnp.maximum(dc, 1e-10)), axis=2)
            cum_decay = jnp.exp(cum_log)
            weighted = vc / jnp.maximum(cum_decay, 1e-10)
            intra_state = cum_decay * jnp.cumsum(weighted, axis=2)
            chunk_final_state = intra_state[:, :, -1, :]
            chunk_total_decay = cum_decay[:, :, -1, :]
            cum_log_chunk = jnp.cumsum(jnp.log(jnp.maximum(chunk_total_decay, 1e-10)), axis=1)
            cum_chunk_decay = jnp.exp(cum_log_chunk)
            cum_weighted_chunk = jnp.cumsum(chunk_final_state / jnp.maximum(cum_chunk_decay, 1e-10), axis=1)
            zeros = jnp.zeros((b, 1, d), dtype=cum_weighted_chunk.dtype)
            ones = jnp.ones((b, 1, d), dtype=cum_chunk_decay.dtype)
            incoming_cum_weighted = jnp.concatenate([zeros, cum_weighted_chunk[:, :-1]], axis=1)
            incoming_cum_decay = jnp.concatenate([ones, cum_chunk_decay[:, :-1]], axis=1)
            incoming_state = incoming_cum_decay * incoming_cum_weighted
            cross_contrib = cum_decay * incoming_state[:, :, None, :]
            states = (intra_state + cross_contrib).reshape(b, total, d)[:, :s]
            return states
        key = jax.random.key(seed)
        k_x, k_w1, k_w2 = jax.random.split(key, 3)
        x = jax.random.normal(k_x, (BATCH, SEQ, D_MODEL), dtype=jnp.float32)
        W_aiv = jax.random.normal(k_w1, (D_MODEL, 3 * D_REC), dtype=jnp.float32) / np.sqrt(D_MODEL)
        decay_bias = _make_decay_bias()
        W_mix = jax.random.normal(k_w2, (D_REC, D_MODEL), dtype=jnp.float32) / np.sqrt(D_REC)
        b_mix = jnp.zeros((D_MODEL,), dtype=jnp.float32)
        return {'x': x, 'W_aiv': W_aiv, 'decay_bias': decay_bias, 'W_mix': W_mix, 'b_mix': b_mix}
    _L0_attn_all = _L0_attn_setup()
    _L0_attn_in = {k: v for k, v in _L0_attn_all.items() if k in ('W_aiv', 'decay_bias', 'W_mix', 'b_mix')}
    del _L0_attn_all

    def _L0_xattn_setup():
        import jax, jax.numpy as jnp
        import numpy as np
        B, S, D, H = (2, 256, 128, 16)
        DK = D // H
        OUT = 128
        key = jax.random.key(seed)
        kq, kk, kv, kl, kw, kb = jax.random.split(key, 6)
        query = jax.random.normal(kq, (B, S, D), dtype=jnp.float32)
        k_ = jax.random.normal(kk, (B, S, D), dtype=jnp.float32)
        v_ = jax.random.normal(kv, (B, S, D), dtype=jnp.float32)
        lengths = jax.random.randint(kl, (B,), S // 2, S + 1)
        mask = (jnp.arange(S)[None, :] < lengths[:, None]).astype(jnp.float32)
        bound = 1.0 / np.sqrt(D)
        Wp = jax.random.uniform(kw, (OUT, D), minval=-bound, maxval=bound, dtype=jnp.float32)
        bp = jax.random.uniform(kb, (OUT,), minval=-bound, maxval=bound, dtype=jnp.float32)
        return {'query': query, 'key': k_, 'value': v_, 'mask': mask, 'Wp': Wp, 'bp': bp}
    _L0_xattn_all = _L0_xattn_setup()
    _L0_xattn_in = {k: v for k, v in _L0_xattn_all.items() if k in ('Wp', 'bp')}
    del _L0_xattn_all

    def _L0_ffn_setup():
        import jax, jax.numpy as jnp
        import numpy as np
        E = 8
        K = 2
        key = jax.random.key(seed)
        ks = jax.random.split(key, 8)
        B, T, d = (4, 256, 128)
        h = 4 * d // E
        s = 0.02
        X = jax.random.normal(ks[0], (B, T, d), jnp.float32)
        routing_W = jax.random.normal(ks[1], (E, d), jnp.float32) * s
        expert_bias = jnp.zeros((E,), jnp.float32)
        sW1 = jax.random.normal(ks[2], (d, h), jnp.float32) * s
        sb1 = jnp.zeros((h,), jnp.float32)
        sW2 = jax.random.normal(ks[3], (h, d), jnp.float32) * s
        sb2 = jnp.zeros((d,), jnp.float32)
        rW1 = jax.random.normal(ks[4], (E, d, h), jnp.float32) * s
        rb1 = jnp.zeros((E, h), jnp.float32)
        rW2 = jax.random.normal(ks[5], (E, h, d), jnp.float32) * s
        rb2 = jnp.zeros((E, d), jnp.float32)
        return dict(X=X, routing_W=routing_W, expert_bias=expert_bias, sW1=sW1, sb1=sb1, sW2=sW2, sb2=sb2, rW1=rW1, rb1=rb1, rW2=rW2, rb2=rb2)
    _L0_ffn_all = _L0_ffn_setup()
    _L0_ffn_in = {k: v for k, v in _L0_ffn_all.items() if k in ('routing_W', 'expert_bias', 'sW1', 'sb1', 'sW2', 'sb2', 'rW1', 'rb1', 'rW2', 'rb2')}
    del _L0_ffn_all
    return {'x': x, 'ctx_1024': ctx_1024, 'mask_BxS2_fk1': mask_BxS2_fk1, 'L0_attn_W_aiv': _L0_attn_in['W_aiv'], 'L0_attn_decay_bias': _L0_attn_in['decay_bias'], 'L0_attn_W_mix': _L0_attn_in['W_mix'], 'L0_attn_b_mix': _L0_attn_in['b_mix'], 'L0_xattn_Wp': _L0_xattn_in['Wp'], 'L0_xattn_bp': _L0_xattn_in['bp'], 'L0_ffn_routing_W': _L0_ffn_in['routing_W'], 'L0_ffn_expert_bias': _L0_ffn_in['expert_bias'], 'L0_ffn_sW1': _L0_ffn_in['sW1'], 'L0_ffn_sb1': _L0_ffn_in['sb1'], 'L0_ffn_sW2': _L0_ffn_in['sW2'], 'L0_ffn_sb2': _L0_ffn_in['sb2'], 'L0_ffn_rW1': _L0_ffn_in['rW1'], 'L0_ffn_rb1': _L0_ffn_in['rb1'], 'L0_ffn_rW2': _L0_ffn_in['rW2'], 'L0_ffn_rb2': _L0_ffn_in['rb2']}

def reference(x, ctx_1024, mask_BxS2_fk1, L0_attn_W_aiv, L0_attn_decay_bias, L0_attn_W_mix, L0_attn_b_mix, L0_xattn_Wp, L0_xattn_bp, L0_ffn_routing_W, L0_ffn_expert_bias, L0_ffn_sW1, L0_ffn_sb1, L0_ffn_sW2, L0_ffn_sb2, L0_ffn_rW1, L0_ffn_rb1, L0_ffn_rW2, L0_ffn_rb2):
    import jax
    import jax.numpy as jnp

    def _L0_attn_ref(x, W_aiv, decay_bias, W_mix, b_mix):
        import jax, jax.numpy as jnp
        import numpy as np
        D_MODEL = 128
        N_HEADS = 16
        D_HEAD = 64
        D_REC = N_HEADS * D_HEAD
        BATCH = 4
        SEQ = 1024
        CHUNK = 64

        def _make_decay_bias():
            n_fast, n_medium, n_slow = (5, 6, 5)
            b = np.zeros(D_REC, dtype=np.float32)
            fast_end = n_fast * D_HEAD
            medium_end = (n_fast + n_medium) * D_HEAD
            b[:fast_end] = -2.2
            b[fast_end:medium_end] = 0.0
            b[medium_end:] = 4.6
            return jnp.asarray(b)

        def _chunked_scan(decay, value, chunk_size=CHUNK):
            b, s, d = decay.shape
            pad = -s % chunk_size
            if pad:
                decay = jnp.pad(decay, ((0, 0), (0, pad), (0, 0)), constant_values=1.0)
                value = jnp.pad(value, ((0, 0), (0, pad), (0, 0)))
            total = s + pad
            n = total // chunk_size
            dc = decay.reshape(b, n, chunk_size, d)
            vc = value.reshape(b, n, chunk_size, d)
            cum_log = jnp.cumsum(jnp.log(jnp.maximum(dc, 1e-10)), axis=2)
            cum_decay = jnp.exp(cum_log)
            weighted = vc / jnp.maximum(cum_decay, 1e-10)
            intra_state = cum_decay * jnp.cumsum(weighted, axis=2)
            chunk_final_state = intra_state[:, :, -1, :]
            chunk_total_decay = cum_decay[:, :, -1, :]
            cum_log_chunk = jnp.cumsum(jnp.log(jnp.maximum(chunk_total_decay, 1e-10)), axis=1)
            cum_chunk_decay = jnp.exp(cum_log_chunk)
            cum_weighted_chunk = jnp.cumsum(chunk_final_state / jnp.maximum(cum_chunk_decay, 1e-10), axis=1)
            zeros = jnp.zeros((b, 1, d), dtype=cum_weighted_chunk.dtype)
            ones = jnp.ones((b, 1, d), dtype=cum_chunk_decay.dtype)
            incoming_cum_weighted = jnp.concatenate([zeros, cum_weighted_chunk[:, :-1]], axis=1)
            incoming_cum_decay = jnp.concatenate([ones, cum_chunk_decay[:, :-1]], axis=1)
            incoming_state = incoming_cum_decay * incoming_cum_weighted
            cross_contrib = cum_decay * incoming_state[:, :, None, :]
            states = (intra_state + cross_contrib).reshape(b, total, d)[:, :s]
            return states
        aiv = x @ W_aiv
        a_proj, i_proj, v = jnp.split(aiv, 3, axis=-1)
        a = jax.nn.sigmoid(a_proj + decay_bias)
        i = jax.nn.sigmoid(i_proj)
        input_signal = jnp.sqrt(jnp.maximum(1.0 - a * a, 1e-08)) * (i * v)
        h = _chunked_scan(a.astype(jnp.float32), input_signal.astype(jnp.float32))
        h = h.astype(x.dtype)
        return h @ W_mix + b_mix

    def _L0_xattn_ref(query, key, value, mask, Wp, bp):
        import jax, jax.numpy as jnp
        import numpy as np
        B, S, D, H = (2, 256, 128, 16)
        DK = D // H
        OUT = 128
        Bsz, Seq, Dm = query.shape
        score_mask = mask[:, :, None] * mask[:, None, :]
        q = query.reshape(Bsz, Seq, H, DK).transpose(0, 2, 1, 3)
        k = key.reshape(Bsz, Seq, H, DK).transpose(0, 2, 1, 3)
        v = value.reshape(Bsz, Seq, H, DK).transpose(0, 2, 1, 3)
        score = jnp.einsum('bhqd,bhkd->bhqk', q, k) / jnp.sqrt(jnp.float32(DK))
        sm = score_mask[:, None, :, :]
        score = jnp.where(sm == 0, jnp.float32(-1000000000.0), score)
        p_attn = jax.nn.softmax(score, axis=-1) * sm
        x = jnp.einsum('bhqk,bhkd->bhqd', p_attn, v)
        x = x.transpose(0, 2, 1, 3).reshape(Bsz, Seq, Dm)
        out = (x @ Wp.T + bp) * mask[:, :, None]
        return out

    def _L0_ffn_ref(X, routing_W, expert_bias, sW1, sb1, sW2, sb2, rW1, rb1, rW2, rb2):
        import jax, jax.numpy as jnp
        import numpy as np
        E = 8
        K = 2
        B, T, d = X.shape
        shared = jax.nn.silu(X @ sW1 + sb1) @ sW2 + sb2
        logits = jnp.einsum('btd,ed->bte', X, routing_W) + expert_bias
        activation = jnp.sqrt(jax.nn.softplus(logits))
        top_vals, top_idx = jax.lax.top_k(activation, K)
        combine = jnp.sum(jax.nn.one_hot(top_idx, E, dtype=X.dtype) * top_vals[..., None], axis=-2)
        Xf = X.reshape(-1, d)
        cf = combine.reshape(-1, E)
        hdn = jax.nn.silu(jnp.einsum('nd,edh->enh', Xf, rW1) + rb1[:, None, :])
        y = jnp.einsum('enh,ehd->end', hdn, rW2) + rb2[:, None, :]
        routed = jnp.einsum('ne,end->nd', cf, y).reshape(B, T, d)
        return shared + routed
    x = _layernorm(x + _L0_attn_ref(x, L0_attn_W_aiv, L0_attn_decay_bias, L0_attn_W_mix, L0_attn_b_mix), axis=-1)
    x = _layernorm(x + _L0_xattn_ref(x, ctx_1024, ctx_1024, mask_BxS2_fk1, L0_xattn_Wp, L0_xattn_bp), axis=-1)
    x = _layernorm(x + _L0_ffn_ref(x, L0_ffn_routing_W, L0_ffn_expert_bias, L0_ffn_sW1, L0_ffn_sb1, L0_ffn_sW2, L0_ffn_sb2, L0_ffn_rW1, L0_ffn_rb1, L0_ffn_rW2, L0_ffn_rb2), axis=-1)
    return x

_drawn_inputs = setup_inputs


def setup_inputs(seed=0):
    import zlib

    import numpy as np

    out = dict(_drawn_inputs(seed))
    spreads = {'L0_attn_b_mix': (0.0, 0.1),
     'L0_ffn_expert_bias': (0.0, 0.1),
     'L0_ffn_sb1': (0.0, 0.8),
     'L0_ffn_sb2': (0.0, 0.1),
     'L0_ffn_rb1': (0.0, 0.77),
     'L0_ffn_rb2': (0.0, 0.1)}
    factors = {'L0_ffn_sW1': 3.143, 'L0_ffn_sW2': 2.912}
    for name, (base, spread) in spreads.items():
        noise = np.random.default_rng([zlib.crc32(name.encode()), seed]).standard_normal(out[name].shape)
        drawn = base * np.exp(spread * noise) if base else spread * noise
        out[name] = jnp.asarray(drawn.astype(out[name].dtype))
    for name, factor in factors.items():
        out[name] = (out[name] * factor).astype(out[name].dtype)
    return out
```

```python
import concourse.bass as bass
from concourse import mybir
from contextlib import ExitStack


def decoder_layer(nc, x, ctx_in, mask, w_aiv, decay_bias, w_mix, b_mix, wp, bp, routing_w,
                  expert_bias, s_w1, s_b1, s_w2, s_b2, r_w1, r_b1, r_w2, r_b2, out):
    F32, BF16, U32 = mybir.dt.float32, mybir.dt.bfloat16, mybir.dt.uint32
    ALU, ACT, AXX = mybir.AluOpType, mybir.ActivationFunctionType, mybir.AxisListType.X

    B, S, D = x.shape
    P = 128
    SEQ_T = P // S
    TILES = B * S // P
    TG = 4
    GROUPS = TILES // TG
    TOK = TG * P
    SEQ_G = TG * SEQ_T
    REC = w_mix.shape[0]
    CT = REC // P
    PAD = S + 1
    LEN = SEQ_G * PAD
    NH = 16
    DK = D // NH
    HH = NH // 2
    PAIRS = HH // 2
    UNITS = 2 * TG
    VC = DK + 1
    E, HID = r_b1.shape
    MT = E * HID // P
    EPS, TINY, CLAMP = 1e-5, 1e-10, 1e-4
    GSTART = 1.0 / TINY
    NEG = -1e9

    with ExitStack() as stack:
        def sb(name, shape, dt=F32):
            return stack.enter_context(nc.sbuf_tensor(name, shape, dt))

        def sem(name):
            return stack.enter_context(nc.semaphore(name))

        x_nat = sb("x_nat", [P, TILES, D])
        ctx_nat = sb("ctx_nat", [P, TILES, D])
        ctx_key = sb("ctx_key", [P, B, D])
        waiv_sb = sb("waiv_sb", [P, 3, REC])
        wmix_sb = sb("wmix_sb", [P, CT, D])
        w1_sb = sb("w1_sb", [P, (E + 1) * HID])
        w2_sb = sb("w2_sb", [P, MT + 1, D])
        b2_sb = sb("b2_sb", [E + 1, D])
        wp_nat = sb("wp_nat", [P, D])
        wpT = sb("wpT", [P, D])
        rw_nat = sb("rw_nat", [E, D])
        rwT = sb("rwT", [P, E])
        NV = CT + MT + 1 + TILES
        R_B1, R_MASK = CT, CT + MT + 1
        vec_rows = sb("vec_rows", [NV, P])
        vec = sb("vec", [P, NV])
        mask_rows = sb("mask_rows", [B, SEQ_T, S])
        mask_key = sb("mask_key", [P, B])
        mask_pair = sb("mask_pair", [SEQ_T, TILES, S])
        key_bias = sb("key_bias", [SEQ_T, TILES, S], BF16)
        row_bias = sb("row_bias", [1, 2 * D + E])
        bias_bc = sb("bias_bc", [P, 2 * D + E])
        ones_row = sb("ones_row", [1, P])
        ident = sb("ident", [P, P])
        kmask = sb("kmask", [P, HH])
        sel = sb("sel", [E + 1, MT, P])
        ind = sb("ind", [SEQ_T, P], BF16)
        iota_i = sb("iota_i", [P, TG * E], mybir.dt.int32)
        iota_f = sb("iota_f", [P, TG, E])
        restart = sb("restart", [P, LEN])

        xT = sb("xT", [P, TILES * P])
        cT = sb("cT", [P, TILES, P])
        a_buf = sb("a_buf", [P, CT, LEN])
        q_buf = sb("q_buf", [P, CT, LEN])
        h_buf = sb("h_buf", [P, CT, LEN])
        iv_buf = sb("iv_buf", [P, CT, TOK])
        r1 = sb("r1", [P, TG, D])
        x1 = sb("x1", [P, TG, D])
        x1T = sb("x1T", [P, TOK])

        kexp = [sb(f"kexp{n}", [P, HH, P]) for n in range(2)]
        v2 = [sb(f"v2{n}", [P, SEQ_T, HH, 2 * VC]) for n in range(2)]
        prob = [sb(f"prob{n}", [P, HH * S]) for n in range(2)]
        probT = [sb(f"probT{n}", [P, HH * S]) for n in range(2)]
        smax = sb("smax", [P, 2, HH])
        mask_q = sb("mask_q", [P, TG])
        rden = sb("rden", [P, 2, NH])
        rdenm = sb("rdenm", [P, 2, NH])
        attn = sb("attn", [P, TG, D])
        attnT = sb("attnT", [P, TOK])
        o_b = sb("o_b", [P, TG, D])
        o_m = sb("o_m", [P, TG, D])
        r2 = sb("r2", [P, TG, D])
        x2 = sb("x2", [P, TG, D])
        x2T = sb("x2T", [P, TOK])
        lg = sb("lg", [P, TG, E])
        top = sb("top", [P, TG, 8])
        top_i = sb("top_i", [P, TG, 8], U32)
        top_f = sb("top_f", [P, TG, 8])
        rt = [sb(f"rt{n}", [P, TG, E]) for n in range(12)]
        cf = sb("cf", [P, TG, E + 1])
        cfT = sb("cfT", [E + 1, TOK])
        hs = sb("hs", [P, MT + 1, TOK])
        hw = ctx_nat[:, :, :].rearrange("p (m t) d -> p m (t d)", m=MT)
        r3 = o_m
        y_out = sb("y_out", [P, TG, D])
        norm_sb = {n: (sb(f"st{n}", [P, TG, 6]), sb(f"mv{n}", [P, TG, 2]),
                       sb(f"ln{n}", [P, TG]), sb(f"rstd{n}", [P, TG])) for n in (1, 2, 3)}

        bank = [stack.enter_context(nc.psum_tensor(f"bank{n}", [P, 512], F32)) for n in range(8)]
        ZA, ZI, ZV, MIX, SC0, SC1, TR, PV = bank

        x_in = [sem(f"x_in{g}") for g in range(GROUPS)]
        ctx_in_s = [sem(f"ctx_in{g}") for g in range(GROUPS)]
        key_in = sem("key_in")
        waiv_in = [sem(f"waiv_in{n}") for n in range(4)]
        small_in = sem("small_in")
        w_in = sem("w_in")
        out_done = sem("out_done")
        ident_made = sem("ident_made")
        const_made = sem("const_made")
        pool_step = sem("pool_step")
        dve_const = sem("dve_const")
        prep_tr = sem("prep_tr")
        prep_copied = sem("prep_copied")
        xb_made = sem("xb_made")
        za_ready, zi_ready, zv_ready = sem("za_ready"), sem("zi_ready"), sem("zv_ready")
        a_made, i_made, a2_made, s_made = sem("a_made"), sem("i_made"), sem("a2_made"), sem("s_made")
        a_clamped, iv_made, g_made = sem("a_clamped"), sem("iv_made"), sem("g_made")
        sig_made, u_made, h_made = sem("sig_made"), sem("u_made"), sem("h_made")
        mix_ready = sem("mix_ready")
        res_made = {n: sem(f"res_made{n}") for n in (1, 2, 3)}
        st_made = {n: sem(f"st_made{n}") for n in (1, 2, 3)}
        mv_made = {n: sem(f"mv_made{n}") for n in (1, 2, 3)}
        ln_made = {n: sem(f"ln_made{n}") for n in (1, 2, 3)}
        rstd_made = {n: sem(f"rstd_made{n}") for n in (1, 2, 3)}
        xn_made = {n: sem(f"xn_made{n}") for n in (1, 2, 3)}
        x1T_ready, x1T_made = sem("x1T_ready"), sem("x1T_made")
        kexp_made, v2_made = sem("kexp_made"), sem("v2_made")
        score_ready, max_made, shifted = sem("score_ready"), sem("max_made"), sem("shifted")
        exp_made, pT_ready, pT_made, pv_ready = sem("exp_made"), sem("pT_ready"), sem("pT_made"), sem("pv_ready")
        rden_made, rdenm_made, attn_made = sem("rden_made"), sem("rdenm_made"), sem("attn_made")
        maskq_made = sem("maskq_made")
        attnT_ready, attnT_made, wp_ready = sem("attnT_ready"), sem("attnT_made"), sem("wp_ready")
        ob_made, om_made = sem("ob_made"), sem("om_made")
        x2T_ready, x2T_made = sem("x2T_ready"), sem("x2T_made")
        lg_ready, lg_made = sem("lg_ready"), sem("lg_made")
        top_made, topi_made, topf_made = sem("top_made"), sem("topi_made"), sem("topf_made")
        nabs_made, expl_made, ln1p_made = sem("nabs_made"), sem("expl_made"), sem("ln1p_made")
        route_step = sem("route_step")
        sp_made, act_made, cf_made = sem("sp_made"), sem("act_made"), sem("cf_made")
        cfT_ready, cfT_made = sem("cfT_ready"), sem("cfT_made")
        cb_ready, hid_ready, silu_made, hw_made = sem("cb_ready"), sem("hid_ready"), sem("silu_made"), sem("hw_made")
        y_ready = sem("y_ready")

        w_in_act = sem("w_in_act")
        kb_made = sem("kb_made")
        pick_step = sem("pick_step")
        eps_col = sb("eps_col", [P, 1])

        PREP = ["vec", "mask", "x0", "wp", "rw", "bias"] + [f"x{g}" for g in range(1, GROUPS)] + \
               [f"c{g}" for g in range(GROUPS)]
        prep_at = lambda name: PREP.index(name) + 1
        prep_bank = lambda n: (SC0, SC1, TR, PV)[n % 4]
        PREP_BIAS, PREP_ALL = prep_at("bias"), len(PREP)
        PREP_X = [prep_at(f"x{g}") for g in range(GROUPS)]
        EARLY = prep_at("x0")
        SMALL = 12
        DVE_CONSTS = 8
        ROUTE = 5
        PICK = 6

        seqs = lambda buf, ct: buf[:, ct, :].rearrange("p (s k) -> p s k", k=PAD)[:, :, 1:PAD]
        flat = lambda ap: ap.rearrange("p t d -> p (t d)")
        toks = lambda ap: ap.rearrange("p (s k) -> p s k", k=S)
        tile = lambda ap, t: ap[:, t * P:(t + 1) * P]

        def head_start(engine, *sems):
            for s in sems:
                engine.sem_inc(s, 1)

        def groups(engine, body):
            body(0, None)
            with engine.Fori(1, GROUPS) as i:
                body(i, i - 1)
            body(None, GROUPS - 1)

        block = stack.enter_context(nc.Block())

        @block.sync
        def _(sp):
            sp.sem_inc(out_done, 16)
            tok = lambda a: a.rearrange("(t b) s d -> (b s) t d", b=SEQ_T)
            w3 = w_aiv.rearrange("d (p c) -> d p c", p=3)
            sp.dma_start(x_nat[:, 0:TG, :], tok(x)[:, 0:TG, :]).then_inc(x_in[0], 16)
            for n in range(4):
                cols = slice(n * REC // 4, (n + 1) * REC // 4)
                sp.dma_start(waiv_sb[:, :, cols], w3[:, :, cols]).then_inc(waiv_in[n], 16)
            for g in range(1, GROUPS):
                ts = slice(g * TG, (g + 1) * TG)
                sp.dma_start(x_nat[:, ts, :], tok(x)[:, ts, :]).then_inc(x_in[g], 16)
            for g in range(GROUPS):
                ts = slice(g * TG, (g + 1) * TG)
                sp.dma_start(ctx_nat[:, ts, :], tok(ctx_in)[:, ts, :]).then_inc(ctx_in_s[g], 16)
            for half in range(2):
                sp.dma_start(ctx_key[half * S:(half + 1) * S, :, :],
                             ctx_in.rearrange("b s d -> s b d")).then_inc(key_in, 16)
            sp.dma_start(w1_sb[:, 0:E * HID].rearrange("d (e h) -> d e h", e=E),
                         r_w1.rearrange("e d h -> d e h")).then_inc(w_in, 16)
            sp.dma_start(w1_sb[:, E * HID:], s_w1).then_inc(w_in, 16)
            sp.dma_start(w2_sb[:, 0:MT, :], r_w2.rearrange("(m e) h d -> (e h) m d", e=2)).then_inc(w_in, 16)
            sp.dma_start(w2_sb[0:HID, MT, :], s_w2).then_inc(w_in, 16)
            sp.dma_start(b2_sb[0:E, :], r_b2).then_inc(w_in, 16)
            sp.dma_start(b2_sb[E:E + 1, :], s_b2.rearrange("(a d) -> a d", a=1)).then_inc(w_in, 16)

            out_t = out.rearrange("(t b) s d -> (b s) t d", b=SEQ_T)

            def store(gA, gB):
                if gB is None:
                    return
                sp.wait_ge(xn_made[3], gB * TG + TG + 1)
                sp.dma_start(out_t[:, bass.ds(gB * TG, TG), :], y_out[:, :, :]).then_inc(out_done, 16)

            with sp.Fori(0, GROUPS) as g:
                store(None, g)
            sp.wait_ge(out_done, 16 * GROUPS + 16)

        @block.gpsimd
        def _(pool):
            head_start(pool, v2_made)
            steps = [0]

            def step(ins):
                steps[0] += 1
                ins.then_inc(pool_step, 1)
                pool.wait_ge(pool_step, steps[0])

            step(nc.gpsimd.memset(ident[:, :], 0.0))
            nc.gpsimd.affine_select(out=ident[:, :], in_=ident[:, :], compare_op=ALU.not_equal, fill=1.0, base=0,
                                    pattern=[[-1, P]], channel_multiplier=1).then_inc(ident_made, 1)
            for half in range(2):
                km = kmask[half * S:(half + 1) * S, :]
                step(nc.gpsimd.memset(km, float(DK) ** -0.5))
                step(nc.gpsimd.affine_select(out=km, in_=km, compare_op=ALU.is_ge, fill=0.0, base=0,
                                             pattern=[[-DK, HH]], channel_multiplier=1))
                step(nc.gpsimd.affine_select(out=km, in_=km, compare_op=ALU.is_ge, fill=0.0, base=DK - 1,
                                             pattern=[[DK, HH]], channel_multiplier=-1))
            step(nc.gpsimd.memset(sel[:, :, :], 0.0))
            nc.gpsimd.affine_select(out=sel[:, :, :].rearrange("e m (b h) -> e m b h", b=2),
                                    in_=sel[:, :, :].rearrange("e m (b h) -> e m b h", b=2),
                                    compare_op=ALU.not_equal, fill=1.0, base=0,
                                    pattern=[[-2, MT], [-1, 2], [0, HID]], channel_multiplier=1).then_inc(const_made, 1)
            step(nc.gpsimd.memset(ind[:, :], 0.0))
            nc.gpsimd.affine_select(out=ind[:, :].rearrange("b (c q) -> b c q", c=SEQ_T),
                                    in_=ind[:, :].rearrange("b (c q) -> b c q", c=SEQ_T),
                                    compare_op=ALU.not_equal, fill=1.0, base=0,
                                    pattern=[[-1, SEQ_T], [0, S]], channel_multiplier=1).then_inc(const_made, 1)
            nc.gpsimd.iota(iota_i[:, :], pattern=[[0, TG], [1, E]], base=0, channel_multiplier=0).then_inc(const_made, 1)
            for n in range(2):
                step(nc.gpsimd.memset(v2[n][:, :, :, :], 0.0))
                step(nc.gpsimd.memset(v2[n][0:S, :, :, DK:VC], 1.0))
                step(nc.gpsimd.memset(v2[n][S:P, :, :, VC + DK:2 * VC], 1.0))
            for g in range(GROUPS):
                pool.wait_ge(prep_copied, PREP_BIAS)
                pool.wait_ge(prep_copied, PREP_X[g])
                xg = x_nat[:, g * TG:(g + 1) * TG, :]
                nc.gpsimd.tensor_tensor(xg, xg, bias_bc[:, None, 0:D].to_broadcast([P, TG, D]),
                                        ALU.add).then_inc(xb_made, 1)
            pool.wait_ge(prep_copied, PREP_ALL)
            pool.wait_ge(key_in, 32)

            with pool.Fori(0, GROUPS) as g:
                for t in range(TG):
                    n = t % 2
                    pool.wait_ge(score_ready, g * UNITS + max(0, 2 * (t - 1)) + 1)
                    pool.wait_ge(v2_made, 2 * (g * TG + t) + 1)
                    nc.gpsimd.tensor_tensor(kexp[n][:, :, :],
                                            cT[:, bass.ds(g * TG + t, 1), :].to_broadcast([P, HH, P]),
                                            kmask[:, :, None].to_broadcast([P, HH, P]), ALU.mult).then_inc(kexp_made, 1)
                    pool.wait_ge(pv_ready, g * UNITS + max(0, 2 * (t - 1)) + 1)
                    pool.wait_ge(kexp_made, g * TG + t + 1)
                    for half in range(2):
                        if half:
                            pool.wait_ge(v2_made, 2 * (g * TG + t) + 1 + 1)
                        rows = slice(half * S, (half + 1) * S)
                        seq = bass.ds((g * TG + t) * SEQ_T, SEQ_T)
                        src = ctx_key[rows, seq, :].rearrange("k b (n h d) -> k b n h d", h=2, d=DK)[:, :, :, half, :]
                        nc.gpsimd.tensor_tensor(v2[n][rows, :, :, half * VC:half * VC + DK], src,
                                                mask_key[rows, seq][:, :, None, None].to_broadcast([S, SEQ_T, HH, DK]),
                                                ALU.mult).then_inc(v2_made, 1)

        @block.tensor
        def _(pe):
            def prep(n):
                name, to = PREP[n], prep_bank(n)
                if n >= 4:
                    pe.wait_ge(prep_copied, n - 3)
                if name == "vec":
                    pe.wait_ge(small_in, 16 * SMALL)
                    pe.wait_ge(dve_const, 1)
                    last = nc.tensor.transpose(to[:, 0:NV], vec_rows[:, :], ident[0:NV, 0:NV])
                elif name == "mask":
                    last = nc.tensor.transpose(to[:, 0:B], mask_rows[:, :, :].rearrange("b c s -> b (c s)"), ident[0:B, 0:B])
                elif name == "wp":
                    last = nc.tensor.transpose(to[:, 0:D], wp_nat[:, :], ident[:, :])
                elif name == "rw":
                    last = nc.tensor.transpose(to[:, 0:E], rw_nat[:, :], ident[0:E, 0:E])
                elif name == "bias":
                    pe.wait_ge(dve_const, 2)
                    last = nc.tensor.matmul(to[:, 0:2 * D + E], ones_row[:, :], row_bias[:, :], start=True, stop=True)
                else:
                    src, came = (x_nat, x_in) if name[0] == "x" else (ctx_nat, ctx_in_s)
                    g = int(name[1:])
                    pe.wait_ge(came[g], 16)
                    for t in range(TG):
                        last = nc.tensor.transpose(tile(to, t), src[:, g * TG + t, :], ident[:, :])
                last.then_inc(prep_tr, 1)

            def project(g, ct):
                if isinstance(g, int):
                    pe.wait_ge(waiv_in[ct // 2], 16)
                for p, (z, ready) in enumerate(((ZA, za_ready), (ZI, zi_ready), (ZV, zv_ready))):
                    if not (isinstance(g, int) and ct == 0):
                        pe.wait_ge((a_made, i_made, iv_made)[p], g * CT + ct)
                    if not isinstance(g, int) and ct == 0:
                        if p < 2:
                            pe.wait_ge(hw_made, (g - 1) * MT + 1)
                        else:
                            pe.wait_ge(res_made[3], g - 1 + 1)
                    nc.tensor.matmul(z[:, :], waiv_sb[:, p, ct * P:(ct + 1) * P], xT[:, bass.ds(g * TOK, TOK)],
                                     start=True, stop=True).then_inc(ready, 1)

            def mix(g, ct):
                pe.wait_ge(h_made, g * CT + ct + 1)
                for s in range(SEQ_G):
                    half, t = s % SEQ_T, s // SEQ_T
                    last = nc.tensor.matmul(MIX[half * S:(half + 1) * S, t * D:(t + 1) * D],
                                            h_buf[:, ct, s * PAD + 1:(s + 1) * PAD], wmix_sb[:, ct, :],
                                            start=(ct == 0 and t == 0), stop=(ct == CT - 1), skip_group_check=True)
                if ct == CT - 1:
                    last.then_inc(mix_ready, 1)

            def scores(g, u):
                t, half = divmod(u, 2)
                to = (SC0, SC1)[half]
                if u == 0:
                    pe.wait_ge(x1T_made, g + 1)
                if half == 0:
                    pe.wait_ge(kexp_made, g * TG + t + 1)
                if u >= 2:
                    pe.wait_ge(shifted, g * UNITS + u - 1)
                else:
                    pe.wait_ge(silu_made, g * (MT + 1) + 1)
                pe.nop(nofuse=True)
                nc.tensor.matmul(to[:, :], ind[:, :],
                                 key_bias[:, bass.ds(g * TG + t, 1), :].to_broadcast([SEQ_T, HH, S]),
                                 start=True, stop=False, skip_group_check=True)
                rows = slice(half * S, (half + 1) * S)
                for b in range(SEQ_T):
                    last = nc.tensor.matmul(to[b * S:(b + 1) * S, :], x1T[rows, t * P + b * S:t * P + (b + 1) * S],
                                            kexp[t % 2][rows, :, b * S:(b + 1) * S],
                                            start=False, stop=True, skip_group_check=True)
                last.then_inc(score_ready, 1)

            def turn_probs(g, u):
                pe.wait_ge(exp_made, g * UNITS + u + 1)
                pe.wait_ge(pT_made, g * UNITS + u + 1)
                for p in range(PAIRS):
                    last = nc.tensor.transpose(tile(TR, p), tile(prob[u % 2], p), ident[:, :])
                last.then_inc(pT_ready, 1)

            def values(g, u):
                t, half = divmod(u, 2)
                pe.wait_ge(pT_made, g * UNITS + u + 1 + 1)
                if half == 0:
                    pe.wait_ge(v2_made, 2 * (g * TG + t + 1) + 1)
                    pe.wait_ge(attn_made, g * TG + t + 1)
                for p in range(PAIRS):
                    pair = half * PAIRS + p
                    for b in range(SEQ_T):
                        last = nc.tensor.matmul(PV[b * S:(b + 1) * S, pair * 2 * VC:(pair + 1) * 2 * VC],
                                                probT[u % 2][:, p * P + b * S:p * P + (b + 1) * S],
                                                v2[t % 2][:, b, pair, :], start=True, stop=True)
                last.then_inc(pv_ready, 1)

            def turn(to, src):
                for t in range(TG):
                    last = nc.tensor.transpose(tile(to, t), src[:, t, :], ident[:, :])
                return last

            def turn_attn(g):
                pe.wait_ge(attn_made, g * TG + TG + 1)
                pe.wait_ge(pT_made, g * UNITS + UNITS + 1)
                turn(TR, attn).then_inc(attnT_ready, 1)

            def out_proj(g):
                pe.wait_ge(attnT_made, g + 1)
                pe.wait_ge(shifted, g * UNITS + UNITS)
                for t in range(TG):
                    last = nc.tensor.matmul(tile(SC0, t), tile(attnT, t), wpT[:, :], start=True, stop=True)
                last.then_inc(wp_ready, 1)

            def turn_x2(g):
                pe.wait_ge(xn_made[2], g * TG + TG + 1)
                turn(SC1, x2).then_inc(x2T_ready, 1)

            def logits(g):
                pe.wait_ge(x2T_made, g + 1)
                for t in range(TG):
                    last = nc.tensor.matmul(TR[:, t * E:(t + 1) * E], tile(x2T, t), rwT[:, :], start=True, stop=True)
                last.then_inc(lg_ready, 1)

            def hidden(g, m):
                width = P if m < MT else HID
                if m == 0:
                    pe.wait_ge(ob_made, g + 1)
                elif m >= 2:
                    pe.wait_ge(silu_made, g * (MT + 1) + m - 1 + 1)
                nc.tensor.matmul((SC0, SC1)[m % 2][0:width, :], w1_sb[:, m * P:m * P + width], x2T[:, :],
                                 start=True, stop=True).then_inc(hid_ready, 1)

            def turn_cf(g):
                pe.wait_ge(cf_made, g + 1)
                for t in range(TG):
                    last = nc.tensor.transpose(TR[0:E + 1, t * P:(t + 1) * P], cf[:, t, :], ident[:, :])
                last.then_inc(cfT_ready, 1)

            def spread_cf(gA, g, m):
                if m == 0:
                    pe.wait_ge(cfT_made, g + 1)
                if m < 2:
                    if gA is not None:
                        pe.wait_ge((a_made, i_made)[m], gA * CT + CT)
                else:
                    pe.wait_ge(hw_made, g * MT + m - 1 + 1)
                nc.tensor.matmul((ZA, ZI)[m % 2][:, :], sel[:, m, :], cfT[:, :], start=True, stop=True).then_inc(cb_ready, 1)

            def experts_out(gA, g):
                if gA is not None:
                    pe.wait_ge(iv_made, gA * CT + CT)
                pe.wait_ge(silu_made, (g + 1) * (MT + 1) + 1)
                pe.wait_ge(hw_made, g * MT + MT + 1)
                for t in range(TG):
                    to = ZV[:, t * D:(t + 1) * D]
                    nc.tensor.matmul(to, tile(cfT, t), b2_sb[:, :], start=True, stop=False)
                    nc.tensor.matmul(to, tile(hs[0:HID, MT, :], t), w2_sb[0:HID, MT, :], start=False, stop=False)
                    for m in range(MT):
                        last = nc.tensor.matmul(to, tile(hw[:, m, :], t), w2_sb[:, m, :], start=False, stop=(m == MT - 1))
                last.then_inc(y_ready, 1)

            def turn_x1(gA, gB):
                pe.wait_ge(xn_made[1], gA * TG + TG + 1)
                if gB is not None:
                    pe.wait_ge(cfT_made, gB + 1)
                else:
                    pe.wait_ge(prep_copied, PREP_ALL)
                turn(TR, x1).then_inc(x1T_ready, 1)

            def iteration(gA, gB):
                A, Bs = gA is not None, gB is not None
                for q in range(TG):
                    if Bs:
                        if q:
                            values(gB, 2 * q - 3) if q > 1 else None
                        scores(gB, 2 * q)
                        scores(gB, 2 * q + 1)
                    if A:
                        project(gA, 2 * q)
                    if Bs and q:
                        turn_probs(gB, 2 * q - 2)
                    if A:
                        project(gA, 2 * q + 1)
                    if Bs and q:
                        turn_probs(gB, 2 * q - 1)
                        values(gB, 2 * q - 2)
                if not Bs:
                    for n in range(EARLY, len(PREP)):
                        prep(n)
                    pe.wait_ge(w_in_act, 16)
                    pe.wait_ge(w_in, 16 * 6)
                    pe.wait_ge(const_made, 3)
                    pe.wait_ge(kb_made, 2)
                if Bs:
                    values(gB, UNITS - 3)
                    turn_probs(gB, UNITS - 2)
                    values(gB, UNITS - 2)
                    turn_probs(gB, UNITS - 1)
                    values(gB, UNITS - 1)
                if A:
                    mix0(gA)
                    mix(gA, 1)
                if Bs:
                    turn_attn(gB)
                if A:
                    mix(gA, 2)
                if Bs:
                    out_proj(gB)
                if A:
                    mix(gA, 3)
                    mix(gA, 4)
                if Bs:
                    turn_x2(gB)
                if A:
                    mix(gA, 5)
                if Bs:
                    logits(gB)
                    hidden(gB, 0)
                    hidden(gB, 1)
                if A:
                    mix(gA, 6)
                    mix(gA, 7)
                if Bs:
                    for m in range(2, MT + 1):
                        hidden(gB, m)
                    turn_cf(gB)
                    for m in range(MT):
                        spread_cf(gA, gB, m)
                    experts_out(gA, gB)
                if A:
                    turn_x1(gA, gB)

            def mix0(g):
                if not isinstance(g, int):
                    pe.wait_ge(res_made[1], g)
                mix(g, 0)

            head_start(pe, score_ready, pT_ready, pv_ready, attnT_ready, x1T_ready)
            pe.wait_ge(ident_made, 1)
            pe.wait_ge(small_in, 16 * SMALL)
            for n in range(EARLY):
                prep(n)
            pe.wait_ge(prep_copied, EARLY)
            groups(pe, iteration)

        @block.scalar
        def _(act):
            head_start(act, silu_made, pT_made, rstd_made[1], rstd_made[2], rstd_made[3])
            row = lambda v: v.rearrange("(a n) -> a n", a=1)
            act.wait_ge(dve_const, 1)
            act.dma_start(vec_rows[0:CT, :], decay_bias.rearrange("(c p) -> c p", p=P)).then_inc(small_in, 16)
            act.dma_start(vec_rows[R_B1:R_B1 + MT, :], r_b1.rearrange("(m e) h -> m (e h)", e=2)).then_inc(small_in, 16)
            act.dma_start(vec_rows[R_B1 + MT:R_B1 + MT + 1, 0:HID], row(s_b1)).then_inc(small_in, 16)
            act.dma_start(vec_rows[R_MASK:NV, :], mask.rearrange("(t b) s -> t (b s)", b=SEQ_T)).then_inc(small_in, 16)
            for c in range(SEQ_T):
                act.dma_start(mask_rows[:, c, :], mask).then_inc(small_in, 16)
            act.dma_start(mask_pair[:, :, :], mask.rearrange("(t b) s -> b t s", b=SEQ_T)).then_inc(small_in, 16)
            act.dma_start(row_bias[:, 0:D], row(b_mix)).then_inc(small_in, 16)
            act.dma_start(row_bias[:, D:2 * D], row(bp)).then_inc(small_in, 16)
            act.dma_start(row_bias[:, 2 * D:], row(expert_bias)).then_inc(small_in, 16)
            act.dma_start(wp_nat[:, :], wp).then_inc(small_in, 16)
            act.dma_start(rw_nat[:, :], routing_w).then_inc(small_in, 16)
            act.dma_start(wmix_sb[:, :, :], w_mix.rearrange("(c p) d -> p c d", p=P)).then_inc(w_in_act, 16)

            def prep_copy(n):
                name, src = PREP[n], prep_bank(n)
                dst = {"vec": vec[:, :], "mask": mask_key[:, :], "wp": wpT[:, :], "rw": rwT[:, :], "bias": bias_bc[:, :]}.get(name)
                if dst is None:
                    g = int(name[1:])
                    dst = xT[:, g * TOK:(g + 1) * TOK] if name[0] == "x" else flat(cT[:, g * TG:(g + 1) * TG, :])
                act.wait_ge(prep_tr, n + 1)
                nc.scalar.activation(dst, src[:, 0:dst.shape[1]], ACT.Copy).then_inc(prep_copied, 1)

            def gates(g, ct):
                first = isinstance(g, int)
                act.wait_ge(za_ready, g * CT + ct + 1)
                if not first:
                    act.wait_ge(h_made, (g - 1) * CT + ct + 1)
                nc.scalar.activation(seqs(a_buf, ct), toks(ZA[:, :]), ACT.Sigmoid, bias=vec[:, ct:ct + 1]).then_inc(a_made, 1)
                act.wait_ge(zi_ready, g * CT + ct + 1)
                if not first:
                    act.wait_ge(sig_made, (g - 1) * CT + ct + 1)
                nc.scalar.activation(iv_buf[:, ct, :], ZI[:, :], ACT.Sigmoid).then_inc(i_made, 1)

            def square(g, ct):
                act.wait_ge(a_clamped, g * CT + ct + 1)
                if not isinstance(g, int):
                    act.wait_ge(h_made, (g - 1) * CT + ct + 1)
                nc.scalar.activation(seqs(q_buf, ct), seqs(a_buf, ct), ACT.Square).then_inc(a2_made, 1)

            def gate_sqrt(g, ct):
                act.wait_ge(a2_made, g * CT + ct + 1)
                nc.scalar.activation(seqs(q_buf, ct), seqs(q_buf, ct), ACT.Sqrt, bias=1.0, scale=-1.0).then_inc(s_made, 1)

            def exps(g, u):
                act.wait_ge(shifted, g * UNITS + u + 1)
                nc.scalar.activation(prob[u % 2][:, :], prob[u % 2][:, :], ACT.Exp).then_inc(exp_made, 1)

            def probs_turned(g, u):
                act.wait_ge(pT_ready, g * UNITS + u + 1 + 1)
                act.wait_ge(pv_ready, g * UNITS + max(0, u - 1) + 1)
                nc.scalar.activation(probT[u % 2][:, :], TR[:, :], ACT.Copy).then_inc(pT_made, 1)

            def rstd(n, g):
                st, mv, ln, rs = norm_sb[n]
                act.wait_ge(mv_made[n], g * TG + TG)
                act.wait_ge(xn_made[n], g * TG + 1)
                nc.scalar.activation(ln[:, :], mv[:, :, 1], ACT.Ln, bias=eps_col[:, :]).then_inc(ln_made[n], 1)
                act.wait_ge(ln_made[n], g + 1)
                nc.scalar.activation(rs[:, :], ln[:, :], ACT.Exp, scale=-0.5).then_inc(rstd_made[n], 1)

            def iteration(gA, gB):
                A, Bs = gA is not None, gB is not None
                for q in range(TG):
                    if A:
                        gates(gA, 2 * q)
                    if Bs and q:
                        probs_turned(gB, 2 * q - 2)
                    if A:
                        gates(gA, 2 * q + 1)
                        square(gA, 2 * q)
                        square(gA, 2 * q + 1)
                    if Bs and q:
                        probs_turned(gB, 2 * q - 1)
                    if Bs:
                        exps(gB, 2 * q)
                        exps(gB, 2 * q + 1)
                if A and not Bs:
                    for ct in range(CT):
                        gate_sqrt(gA, ct)
                    for n in range(EARLY, len(PREP)):
                        prep_copy(n)
                if Bs:
                    probs_turned(gB, UNITS - 2)
                    probs_turned(gB, UNITS - 1)
                    if A:
                        for ct in range(4):
                            gate_sqrt(gA, ct)
                    act.wait_ge(attnT_ready, gB + 1 + 1)
                    nc.scalar.activation(attnT[:, :], TR[:, :], ACT.Copy).then_inc(attnT_made, 1)
                    if A:
                        for ct in range(4, CT):
                            gate_sqrt(gA, ct)
                    rstd(2, gB)
                    act.wait_ge(x2T_ready, gB + 1)
                    nc.scalar.activation(x2T[:, :], SC1[:, :], ACT.Copy).then_inc(x2T_made, 1)
                    act.wait_ge(nabs_made, gB + 1)
                    nc.scalar.activation(rt[1][:, :, :], rt[0][:, :, :], ACT.Exp).then_inc(expl_made, 1)
                    act.wait_ge(route_step, gB * ROUTE + 1)
                    nc.scalar.activation(rt[3][:, :, :], rt[2][:, :, :], ACT.Ln).then_inc(ln1p_made, 1)
                    act.wait_ge(sp_made, gB + 1)
                    nc.scalar.activation(rt[9][:, :, :], rt[8][:, :, :], ACT.Sqrt).then_inc(act_made, 1)
                    for m in range(2):
                        silu(gB, m)
                    for m in range(2, MT + 1):
                        silu(gB, m)
                    act.wait_ge(cfT_ready, gB + 1)
                    nc.scalar.activation(cfT[:, :], TR[0:E + 1, :], ACT.Copy).then_inc(cfT_made, 1)
                if A:
                    rstd(1, gA)
                    act.wait_ge(x1T_ready, gA + 1 + 1)
                    nc.scalar.activation(x1T[:, :], TR[:, :], ACT.Copy).then_inc(x1T_made, 1)
                if Bs:
                    rstd(3, gB)

            def silu(g, m):
                width = P if m < MT else HID
                act.wait_ge(hid_ready, g * (MT + 1) + m + 1)
                nc.scalar.activation(hs[0:width, m, :], (SC0, SC1)[m % 2][0:width, :], ACT.Silu,
                                     bias=vec[0:width, R_B1 + m:R_B1 + m + 1]).then_inc(silu_made, 1)

            for n in range(EARLY):
                prep_copy(n)
            act.wait_ge(prep_copied, EARLY)
            act.wait_ge(dve_const, DVE_CONSTS)
            groups(act, iteration)

        @block.vector
        def _(dve):
            head_start(dve, attn_made, hw_made, res_made[3], xn_made[1], xn_made[2], xn_made[3])
            nc.vector.memset(vec_rows[:, :], 0.0).then_inc(dve_const, 1)
            nc.vector.memset(ones_row[:, :], 1.0).then_inc(dve_const, 1)
            nc.vector.memset(eps_col[:, :], EPS).then_inc(dve_const, 1)
            nc.vector.memset(cf[:, :, E:], 1.0).then_inc(dve_const, 1)
            pads = lambda buf: buf.rearrange("p (s k) -> p s k", k=PAD)[:, :, 0]
            nc.vector.memset(restart[:, :], 0.0).then_inc(dve_const, 1)
            nc.vector.memset(a_buf[:, :, :].rearrange("p c (s k) -> p (c s) k", k=PAD)[:, :, 0], 0.0).then_inc(dve_const, 1)
            nc.vector.memset(q_buf[:, :, :].rearrange("p c (s k) -> p (c s) k", k=PAD)[:, :, 0], 0.0).then_inc(dve_const, 1)
            dve.wait_ge(dve_const, 5)
            nc.vector.memset(pads(restart[:, :]), GSTART).then_inc(dve_const, 1)
            dve.wait_ge(small_in, 16 * SMALL)
            nc.vector.tensor_scalar(key_bias[:, :, :], mask_pair[:, :, :], 0.0, NEG, ALU.is_equal, ALU.mult).then_inc(kb_made, 1)
            dve.wait_ge(const_made, 3)
            nc.vector.tensor_copy(flat(iota_f[:, :, :]), iota_i[:, :]).then_inc(kb_made, 1)
            dve.wait_ge(dve_const, DVE_CONSTS)
            dve.wait_ge(kb_made, 2)

            def scan_decay(g, ct):
                dve.wait_ge(a_made, g * CT + ct + 1)
                nc.vector.tensor_scalar(seqs(a_buf, ct), seqs(a_buf, ct), TINY, 1.0, ALU.max, ALU.min).then_inc(a_clamped, 1)
                dve.wait_ge(i_made, g * CT + ct + 1)
                dve.wait_ge(zv_ready, g * CT + ct + 1)
                nc.vector.tensor_tensor(iv_buf[:, ct, :], ZV[:, :], iv_buf[:, ct, :], ALU.mult).then_inc(iv_made, 1)
                dve.wait_ge(a_clamped, g * CT + ct + 1)
                if not isinstance(g, int) and ct == 0:
                    dve.wait_ge(mix_ready, g)
                nc.vector.tensor_tensor_scan(h_buf[:, ct, :], a_buf[:, ct, :], restart[:, :], 0.0,
                                             ALU.mult, ALU.add).then_inc(g_made, 1)

            def scan_state(g, ct):
                at = g * CT + ct + 1
                dve.wait_ge(s_made, at)
                dve.wait_ge(iv_made, at)
                nc.vector.scalar_tensor_tensor(seqs(q_buf, ct), seqs(q_buf, ct), CLAMP, toks(iv_buf[:, ct, :]),
                                               ALU.max, ALU.mult).then_inc(sig_made, 1)
                dve.wait_ge(sig_made, at)
                dve.wait_ge(g_made, at)
                nc.vector.scalar_tensor_tensor(q_buf[:, ct, :], h_buf[:, ct, :], 1.0, q_buf[:, ct, :],
                                               ALU.min, ALU.mult).then_inc(u_made, 1)
                dve.wait_ge(u_made, at)
                nc.vector.tensor_tensor_scan(h_buf[:, ct, :], a_buf[:, ct, :], q_buf[:, ct, :], 0.0,
                                             ALU.mult, ALU.add).then_inc(h_made, 1)

            def shift(g, u):
                to = (SC0, SC1)[u % 2]
                s3 = lambda a: a.rearrange("p (h k) -> p h k", k=S)
                dve.wait_ge(score_ready, g * UNITS + u + 1 + 1)
                nc.vector.tensor_reduce(smax[:, u % 2, :], s3(to[:, :]), AXX, ALU.max).then_inc(max_made, 1)
                dve.wait_ge(max_made, g * UNITS + u + 1)
                dve.wait_ge(pT_ready, g * UNITS + max(0, u - 1) + 1)
                nc.vector.tensor_tensor(s3(prob[u % 2][:, :]), s3(to[:, :]),
                                        smax[:, u % 2, :].unsqueeze(2).to_broadcast([P, HH, S]),
                                        ALU.subtract).then_inc(shifted, 1)

            def attend(g, t):
                pv = PV[:, 0:NH * VC].rearrange("p (h c) -> p h c", c=VC)
                dve.wait_ge(pv_ready, g * UNITS + 2 * t + 2 + 1)
                nc.vector.reciprocal(rden[:, t % 2, :], pv[:, :, DK]).then_inc(rden_made, 1)
                dve.wait_ge(rden_made, g * TG + t + 1)
                dve.wait_ge(maskq_made, g + 1)
                nc.vector.tensor_scalar(rdenm[:, t % 2, :], rden[:, t % 2, :], mask_q[:, t:t + 1], None,
                                        ALU.mult).then_inc(rdenm_made, 1)
                dve.wait_ge(rdenm_made, g * TG + t + 1)
                if t == 0:
                    dve.wait_ge(attnT_ready, g + 1)
                nc.vector.tensor_tensor(attn[:, t, :].rearrange("p (h c) -> p h c", c=DK), pv[:, :, 0:DK],
                                        rdenm[:, t % 2, :].unsqueeze(2).to_broadcast([P, NH, DK]),
                                        ALU.mult).then_inc(attn_made, 1)

            def stats(n, g, r):
                st, mv, ln, rs = norm_sb[n]
                dve.wait_ge(res_made[n], g + (2 if n == 3 else 1))
                for t in range(TG):
                    nc.vector.bn_stats(st[:, t, :], r[:, t, :]).then_inc(st_made[n], 1)
                dve.wait_ge(rstd_made[n], g + 1)
                for t in range(TG):
                    dve.wait_ge(st_made[n], g * TG + t + 1)
                    dve.nop(nofuse=True)
                    nc.vector.bn_aggr(mv[:, t, :], st[:, t, :]).then_inc(mv_made[n], 1)

            def normalise(n, g, r, xn):
                st, mv, ln, rs = norm_sb[n]
                dve.wait_ge(rstd_made[n], g + 1 + 1)
                for t in range(TG):
                    nc.vector.tensor_scalar(xn[:, t, :], r[:, t, :], mv[:, t, 0:1], rs[:, t:t + 1],
                                            ALU.subtract, ALU.mult).then_inc(xn_made[n], 1)

            def residual1(g):
                dve.wait_ge(mix_ready, g + 1)
                dve.wait_ge(xb_made, g + 1)
                nc.vector.tensor_tensor(flat(r1[:, :, :]), MIX[:, :],
                                        x_nat[:, bass.ds(g * TG, TG), :].rearrange("p t d -> p (t d)"),
                                        ALU.add).then_inc(res_made[1], 1)
                stats(1, g, r1)

            def norm1(gA, gB):
                if gB is None:
                    pass
                dve.wait_ge(x1T_ready, gA + 1)
                normalise(1, gA, r1, x1)

            def residual2(g):
                dve.wait_ge(wp_ready, g + 1)
                nc.vector.tensor_tensor(o_b[:, :, :], SC0[:, :].rearrange("p (t d) -> p t d", d=D),
                                        bias_bc[:, None, D:2 * D].to_broadcast([P, TG, D]), ALU.add).then_inc(ob_made, 1)
                dve.wait_ge(ob_made, g + 1)
                nc.vector.tensor_tensor(o_m[:, :, :], o_b[:, :, :], mask_q[:, :].unsqueeze(2).to_broadcast([P, TG, D]),
                                        ALU.mult).then_inc(om_made, 1)
                dve.wait_ge(om_made, g + 1)
                nc.vector.tensor_tensor(r2[:, :, :], o_m[:, :, :], x1[:, :, :], ALU.add).then_inc(res_made[2], 1)
                stats(2, g, r2)

            def route_logits(g):
                dve.wait_ge(lg_ready, g + 1)
                nc.vector.tensor_tensor(lg[:, :, :], TR[:, 0:TG * E].rearrange("p (t e) -> p t e", e=E),
                                        bias_bc[:, None, 2 * D:].to_broadcast([P, TG, E]), ALU.add).then_inc(lg_made, 1)
                dve.wait_ge(lg_made, g + 1)
                nc.vector.scalar_tensor_tensor(rt[0][:, :, :], lg[:, :, :], -1.0, lg[:, :, :], ALU.mult, ALU.min).then_inc(nabs_made, 1)
                for t in range(TG):
                    nc.vector.max(top[:, t, :], lg[:, t, :]).then_inc(top_made, 1)
                for t in range(TG):
                    dve.wait_ge(top_made, g * TG + t + 1)
                    dve.nop(nofuse=True)
                    nc.vector.max_index(top_i[:, t, :], top[:, t, :], lg[:, t, :]).then_inc(topi_made, 1)
                dve.wait_ge(topi_made, g * TG + TG)
                nc.vector.tensor_copy(top_f[:, :, :], top_i[:, :, :]).then_inc(topf_made, 1)
                dve.wait_ge(expl_made, g + 1)
                nc.vector.tensor_scalar(rt[2][:, :, :], rt[1][:, :, :], 1.0, None, ALU.add).then_inc(route_step, 1)

            def route_combine(g):
                step = lambda n: dve.wait_ge(route_step, g * ROUTE + n)
                e, u, dlt, dg, rc = rt[1], rt[2], rt[4], rt[5], rt[6]
                step(1)
                nc.vector.tensor_scalar(dlt[:, :, :], u[:, :, :], 1.0, None, ALU.subtract).then_inc(route_step, 1)
                nc.vector.tensor_scalar(rt[11][:, :, :], u[:, :, :], 1.0, None, ALU.is_equal).then_inc(route_step, 1)
                step(2)
                nc.vector.tensor_scalar(dg[:, :, :], dlt[:, :, :], 1e-30, None, ALU.max).then_inc(route_step, 1)
                step(4)
                nc.vector.reciprocal(rc[:, :, :], dg[:, :, :]).then_inc(route_step, 1)
                dve.wait_ge(topf_made, g + 1)
                pick = lambda n: top_f[:, :, n:n + 1].to_broadcast([P, TG, E])
                nc.vector.tensor_tensor(rt[10][:, :, :], iota_f[:, :, :], pick(0), ALU.is_equal).then_inc(pick_step, 1)
                nc.vector.tensor_tensor(rt[7][:, :, :], iota_f[:, :, :], pick(1), ALU.is_equal).then_inc(pick_step, 1)
                dve.wait_ge(pick_step, g * PICK + 2)
                nc.vector.tensor_tensor(rt[10][:, :, :], rt[10][:, :, :], rt[7][:, :, :], ALU.add).then_inc(pick_step, 1)
                dve.wait_ge(ln1p_made, g + 1)
                step(5)
                nc.vector.tensor_tensor(rt[3][:, :, :], rt[3][:, :, :], rc[:, :, :], ALU.mult).then_inc(pick_step, 1)
                dve.wait_ge(pick_step, g * PICK + 4)
                nc.vector.tensor_tensor(rt[3][:, :, :], rt[3][:, :, :], rt[11][:, :, :], ALU.add).then_inc(pick_step, 1)
                dve.wait_ge(pick_step, g * PICK + 5)
                nc.vector.tensor_tensor(rt[3][:, :, :], rt[3][:, :, :], e[:, :, :], ALU.mult).then_inc(pick_step, 1)
                dve.wait_ge(pick_step, g * PICK + 6)
                nc.vector.scalar_tensor_tensor(rt[8][:, :, :], lg[:, :, :], 0.0, rt[3][:, :, :], ALU.max, ALU.add).then_inc(sp_made, 1)
                dve.wait_ge(act_made, g + 1)
                nc.vector.tensor_tensor(cf[:, :, 0:E], rt[9][:, :, :], rt[10][:, :, :], ALU.mult).then_inc(cf_made, 1)

            def weigh(g, m):
                dve.wait_ge(cb_ready, g * MT + m + 1)
                dve.wait_ge(silu_made, g * (MT + 1) + m + 1 + 1)
                nc.vector.tensor_tensor(hw[:, m, :], (ZA, ZI)[m % 2][:, :], hs[:, m, :], ALU.mult).then_inc(hw_made, 1)

            def residual3(g):
                dve.wait_ge(y_ready, g + 1)
                nc.vector.tensor_tensor(flat(r3[:, :, :]), ZV[:, :], flat(x2[:, :, :]), ALU.add).then_inc(res_made[3], 1)
                stats(3, g, r3)

            def norm3(g):
                dve.wait_ge(out_done, 16 * g + 16)
                normalise(3, g, r3, y_out)

            def iteration(gA, gB):
                A, Bs = gA is not None, gB is not None
                if Bs:
                    dve.wait_ge(prep_copied, PREP_ALL)
                    nc.vector.tensor_copy(mask_q[:, :], vec[:, bass.ds(R_MASK + gB * TG, TG)]).then_inc(maskq_made, 1)
                for q in range(TG):
                    for ct in (2 * q, 2 * q + 1):
                        if A:
                            scan_decay(gA, ct)
                        if Bs:
                            shift(gB, ct)
                    if Bs and q >= 2:
                        attend(gB, q - 2)
                if Bs:
                    attend(gB, 2)
                if A:
                    scan_state(gA, 0)
                    scan_state(gA, 1)
                if Bs:
                    attend(gB, 3)
                if A:
                    scan_state(gA, 2)
                    scan_state(gA, 3)
                if Bs:
                    residual2(gB)
                if A:
                    scan_state(gA, 4)
                if Bs:
                    normalise(2, gB, r2, x2)
                if A:
                    scan_state(gA, 5)
                    scan_state(gA, 6)
                if Bs:
                    route_logits(gB)
                if A:
                    scan_state(gA, 7)
                if Bs:
                    route_combine(gB)
                if A:
                    residual1(gA)
                if Bs:
                    for m in range(MT):
                        weigh(gB, m)
                if A:
                    norm1(gA, gB)
                if Bs:
                    residual3(gB)
                    norm3(gB)

            groups(dve, iteration)


_INS = ['x', 'ctx_1024', 'mask_BxS2_fk1', 'L0_attn_W_aiv', 'L0_attn_decay_bias', 'L0_attn_W_mix',
        'L0_attn_b_mix', 'L0_xattn_Wp', 'L0_xattn_bp', 'L0_ffn_routing_W', 'L0_ffn_expert_bias',
        'L0_ffn_sW1', 'L0_ffn_sb1', 'L0_ffn_sW2', 'L0_ffn_sb2', 'L0_ffn_rW1', 'L0_ffn_rb1',
        'L0_ffn_rW2', 'L0_ffn_rb2']
_OUTS = [((32, 64, 128), 'float32')]


def kernel(**inputs):
    import numpy as _np
    import concourse.bacc as _bacc
    from concourse import mybir as _mybir
    from concourse.bass_utils import run_bass_kernel_spmd as _run

    nc = _bacc.Bacc("TRN2", target_bir_lowering=False, num_devices=1)
    arrays, args = {}, []
    for name in _INS:
        a = _np.ascontiguousarray(inputs[name])
        arrays[f"in_{name}_dram"] = a
        args.append(nc.dram_tensor(f"in_{name}_dram", a.shape, _mybir.dt.from_np(a.dtype), kind="ExternalInput").ap())
    for i, (shape, dtype) in enumerate(_OUTS):
        dt = _mybir.dt.from_np(_np.dtype(dtype))
        args.append(nc.dram_tensor(f"out_{i}_dram", shape, dt, kind="ExternalOutput").ap())
    decoder_layer(nc, *args)
    r = _run(nc, [arrays], core_ids=[0])
    return r.results[0]["out_0_dram"]
```

```python
import concourse.bass as bass
from concourse import mybir
from contextlib import ExitStack


def decoder_layer(nc, x, ctx_in, mask, w_aiv, decay_bias, w_mix, b_mix, wp, bp, routing_w,
                  expert_bias, s_w1, s_b1, s_w2, s_b2, r_w1, r_b1, r_w2, r_b2, out):
    F32, BF16, U32 = mybir.dt.float32, mybir.dt.bfloat16, mybir.dt.uint32
    ALU, ACT, AXX = mybir.AluOpType, mybir.ActivationFunctionType, mybir.AxisListType.X

    B, S, D = x.shape
    P = 128
    SEQ_T = P // S
    TILES = B * S // P
    TG = 4
    GROUPS = TILES // TG
    TOK = TG * P
    SEQ_G = TG * SEQ_T
    REC = w_mix.shape[0]
    CT = REC // P
    PAD = S + 1
    LEN = SEQ_G * PAD
    NH = 16
    DK = D // NH
    HH = NH // 2
    PAIRS = HH // 2
    UNITS = 2 * TG
    VC = DK + 1
    E, HID = r_b1.shape
    MT = E * HID // P
    EPS, TINY, CLAMP = 1e-5, 1e-10, 1e-4
    GSTART = 1.0 / TINY
    NEG = -1e9

    with ExitStack() as stack:
        def sb(name, shape, dt=F32):
            return stack.enter_context(nc.sbuf_tensor(name, shape, dt))

        def sem(name):
            return stack.enter_context(nc.semaphore(name))

        x_nat = sb("x_nat", [P, TILES, D])
        ctx_nat = sb("ctx_nat", [P, TILES, D])
        ctx_key = sb("ctx_key", [P, B, D])
        waiv_sb = sb("waiv_sb", [P, 3, REC])
        wmix_sb = sb("wmix_sb", [P, CT, D])
        w1_sb = sb("w1_sb", [P, (E + 1) * HID])
        w2_sb = sb("w2_sb", [P, MT + 1, D])
        b2_sb = sb("b2_sb", [P, D])
        wp_nat = sb("wp_nat", [P, D])
        wpT = sb("wpT", [P, D])
        rw_nat = sb("rw_nat", [E, D])
        rwT = sb("rwT", [P, E])
        NV = CT + MT + 1 + TILES
        R_B1, R_MASK = CT, CT + MT + 1
        vec_rows = sb("vec_rows", [NV, P])
        vec = sb("vec", [P, NV])
        mask_rows = sb("mask_rows", [B, SEQ_T, S])
        mask_key = sb("mask_key", [P, B])
        mask_pair = sb("mask_pair", [SEQ_T, TILES, S])
        key_bias = sb("key_bias", [P, TILES, S], BF16)
        row_bias = sb("row_bias", [P, 2 * D + E])
        bias_bc = sb("bias_bc", [P, 2 * D + E])
        ones_row = sb("ones_row", [P, P])
        ident = sb("ident", [P, P])
        kmask = sb("kmask", [P, HH])
        sel = sb("sel", [P, MT, P])
        ind = sb("ind", [P, P], BF16)
        iota_i = sb("iota_i", [P, TG * E], mybir.dt.int32)
        iota_f = sb("iota_f", [P, TG, E])
        restart = sb("restart", [P, LEN])

        xT = sb("xT", [P, TILES * P])
        cT = sb("cT", [P, TILES, P])
        a_buf = sb("a_buf", [P, CT, LEN])
        q_buf = sb("q_buf", [P, CT, LEN])
        h_buf = sb("h_buf", [P, CT, LEN])
        iv_buf = sb("iv_buf", [P, CT, TOK])
        r1 = sb("r1", [P, TG, D])
        x1 = r1
        x1T = sb("x1T", [P, TOK])
        mixT = x1T

        kexp = [sb(f"kexp{n}", [P, HH, P]) for n in range(2)]
        v2 = [sb(f"v2{n}", [P, SEQ_T, HH, 2 * VC]) for n in range(TG)]
        PB = 4
        prob = [sb(f"prob{n}", [P, HH * S]) for n in range(PB)]
        probT = [sb(f"probT{n}", [P, HH * S]) for n in range(2)]
        smax = sb("smax", [P, 2, HH])
        mask_q = sb("mask_q", [P, TG])
        rden = sb("rden", [P, 2, NH])
        rdenm = sb("rdenm", [P, 2, NH])
        attn = sb("attn", [P, TG, D])
        attnT = sb("attnT", [P, TOK])
        r2 = sb("r2", [P, TG, D])
        x2 = sb("x2", [P, TG, D])
        x2T = sb("x2T", [P, TOK])
        lg = sb("lg", [P, TG, E])
        top = sb("top", [P, TG, 8])
        top_i = sb("top_i", [P, TG, 8], U32)
        top_f = sb("top_f", [P, TG, 8])
        rt = [sb(f"rt{n}", [P, TG, E]) for n in range(12)]
        cf = sb("cf", [P, TG, E + 1])
        cfT = sb("cfT", [P, TOK])
        hs = sb("hs", [P, MT + 1, TOK])
        hw = ctx_nat[:, :, :].rearrange("p (m t) d -> p m (t d)", m=MT)
        r3 = sb("r3", [P, TG, D])
        y_out = r3
        norm_sb = {n: (sb(f"st{n}", [P, TG, 6]), sb(f"mv{n}", [P, TG, 2]),
                       sb(f"ln{n}", [P, TG]), sb(f"rstd{n}", [P, TG])) for n in (1, 2, 3)}

        bank = [stack.enter_context(nc.psum_tensor(f"bank{n}", [P, 512], F32)) for n in range(8)]
        ZA, ZI, ZV, SC, TR, PV, CB, MX = bank

        x_in = [sem(f"x_in{g}") for g in range(GROUPS)]
        ctx_in_s = [sem(f"ctx_in{g}") for g in range(GROUPS)]
        key_in = sem("key_in")
        waiv_in = [sem(f"waiv_in{n}") for n in range(4)]
        small_in = sem("small_in")
        w_in = sem("w_in")
        out_done = sem("out_done")
        ident_made = sem("ident_made")
        const_made = sem("const_made")
        pool_step = sem("pool_step")
        dve_const = sem("dve_const")
        prep_tr = sem("prep_tr")
        prep_copied = sem("prep_copied")
        xb_made = sem("xb_made")
        za_ready, zi_ready, zv_ready = sem("za_ready"), sem("zi_ready"), sem("zv_ready")
        a_made, i_made, a2_made, s_made = sem("a_made"), sem("i_made"), sem("a2_made"), sem("s_made")
        a_clamped, iv_made, g_made = sem("a_clamped"), sem("iv_made"), sem("g_made")
        sig_made, u_made, h_made = sem("sig_made"), sem("u_made"), sem("h_made")
        mix_ready, mixT_made, mix_turned = sem("mix_ready"), sem("mixT_made"), sem("mix_turned")
        res_made = {n: sem(f"res_made{n}") for n in (1, 2, 3)}
        st_made = {n: sem(f"st_made{n}") for n in (1, 2, 3)}
        mv_made = {n: sem(f"mv_made{n}") for n in (1, 2, 3)}
        dev_made = {n: sem(f"dev_made{n}") for n in (1, 2, 3)}
        rstd_made = {n: sem(f"rstd_made{n}") for n in (1, 2, 3)}
        xn_made = {n: sem(f"xn_made{n}") for n in (1, 2, 3)}
        x1T_ready, x1T_made = sem("x1T_ready"), sem("x1T_made")
        kexp_made, v2_made = sem("kexp_made"), sem("v2_made")
        score_ready, max_made, shifted = sem("score_ready"), sem("max_made"), sem("shifted")
        exp_made, pT_ready, pT_made, pv_ready = sem("exp_made"), sem("pT_ready"), sem("pT_made"), sem("pv_ready")
        rden_made, rdenm_made, attn_made = sem("rden_made"), sem("rdenm_made"), sem("attn_made")
        maskq_made = sem("maskq_made")
        attnT_ready, attnT_made, wp_ready = sem("attnT_ready"), sem("attnT_made"), sem("wp_ready")
        x2T_ready, x2T_made = sem("x2T_ready"), sem("x2T_made")
        lg_ready, lg_made = sem("lg_ready"), sem("lg_made")
        top_made, topi_made, topf_made = sem("top_made"), sem("topi_made"), sem("topf_made")
        nabs_made, expl_made, ln1p_made = sem("nabs_made"), sem("expl_made"), sem("ln1p_made")
        route_step = sem("route_step")
        sp_made, act_made, cf_made = sem("sp_made"), sem("act_made"), sem("cf_made")
        cfT_ready, cfT_made = sem("cfT_ready"), sem("cfT_made")
        cb_ready, hid_ready, silu_made, hw_made = sem("cb_ready"), sem("hid_ready"), sem("silu_made"), sem("hw_made")
        y_ready = sem("y_ready")

        w_in_act = sem("w_in_act")
        kb_made = sem("kb_made")
        pick_step = sem("pick_step")
        eps_col = sb("eps_col", [P, 1])

        PREP = ["vec", "mask", "x0", "wp", "rw", "bias"] + [f"x{g}" for g in range(1, GROUPS)] + \
               [f"c{g}" for g in range(GROUPS)]
        prep_at = lambda name: PREP.index(name) + 1
        prep_bank = lambda n: (SC, MX, TR, PV)[n % 4]
        PREP_BIAS, PREP_ALL = prep_at("bias"), len(PREP)
        PREP_X = [prep_at(f"x{g}") for g in range(GROUPS)]
        EARLY = prep_at("x0")
        SMALL = 12
        DVE_CONSTS = 13
        ROUTE = 5
        PICK = 6

        seqs = lambda buf, ct: buf[:, ct, :].rearrange("p (s k) -> p s k", k=PAD)[:, :, 1:PAD]
        flat = lambda ap: ap.rearrange("p t d -> p (t d)")
        toks = lambda ap: ap.rearrange("p (s k) -> p s k", k=S)
        tile = lambda ap, t: ap[:, t * P:(t + 1) * P]

        def head_start(engine, *sems):
            for s in sems:
                engine.sem_inc(s, 1)

        def groups(body, engine):
            body(0, None, None)
            body(1, 0, None)
            with engine.Fori(2, GROUPS) as i:
                body(i, i - 1, i - 2)
            body(None, GROUPS - 1, GROUPS - 2)
            body(None, None, GROUPS - 1)

        first = lambda g: isinstance(g, int) and g == 0

        block = stack.enter_context(nc.Block())

        @block.sync
        def _(sp):
            sp.sem_inc(out_done, 16)
            tok = lambda a: a.rearrange("(t b) s d -> (b s) t d", b=SEQ_T)
            w3 = w_aiv.rearrange("d (p c) -> d p c", p=3)
            sp.dma_start(x_nat[:, 0:TG, :], tok(x)[:, 0:TG, :]).then_inc(x_in[0], 16)
            for n in range(4):
                cols = slice(n * REC // 4, (n + 1) * REC // 4)
                sp.dma_start(waiv_sb[:, :, cols], w3[:, :, cols]).then_inc(waiv_in[n], 16)
            for g in range(1, GROUPS):
                ts = slice(g * TG, (g + 1) * TG)
                sp.dma_start(x_nat[:, ts, :], tok(x)[:, ts, :]).then_inc(x_in[g], 16)
            for g in range(GROUPS):
                ts = slice(g * TG, (g + 1) * TG)
                sp.dma_start(ctx_nat[:, ts, :], tok(ctx_in)[:, ts, :]).then_inc(ctx_in_s[g], 16)
            for half in range(2):
                sp.dma_start(ctx_key[half * S:(half + 1) * S, :, :],
                             ctx_in.rearrange("b s d -> s b d")).then_inc(key_in, 16)
            sp.dma_start(w1_sb[:, 0:E * HID].rearrange("d (e h) -> d e h", e=E),
                         r_w1.rearrange("e d h -> d e h")).then_inc(w_in, 16)
            sp.dma_start(w1_sb[:, E * HID:], s_w1).then_inc(w_in, 16)
            sp.dma_start(w2_sb[:, 0:MT, :], r_w2.rearrange("(m e) h d -> (e h) m d", e=2)).then_inc(w_in, 16)
            sp.dma_start(w2_sb[0:HID, MT, :], s_w2).then_inc(w_in, 16)
            sp.wait_ge(dve_const, 4)
            sp.dma_start(b2_sb[0:E, :], r_b2).then_inc(w_in, 16)
            sp.dma_start(b2_sb[E:E + 1, :], s_b2.rearrange("(a d) -> a d", a=1)).then_inc(w_in, 16)

            out_t = out.rearrange("(t b) s d -> (b s) t d", b=SEQ_T)

            with sp.Fori(0, GROUPS) as g:
                sp.wait_ge(xn_made[3], g * TG + TG + 1)
                sp.dma_start(out_t[:, bass.ds(g * TG, TG), :], y_out[:, :, :]).then_inc(out_done, 16)
            sp.wait_ge(out_done, 16 * GROUPS + 16)

        @block.gpsimd
        def _(pool):
            head_start(pool, v2_made)
            steps = [0]

            def step(ins):
                steps[0] += 1
                ins.then_inc(pool_step, 1)
                pool.wait_ge(pool_step, steps[0])

            step(nc.gpsimd.memset(ident[:, :], 0.0))
            nc.gpsimd.affine_select(out=ident[:, :], in_=ident[:, :], compare_op=ALU.not_equal, fill=1.0, base=0,
                                    pattern=[[-1, P]], channel_multiplier=1).then_inc(ident_made, 1)
            for half in range(2):
                km = kmask[half * S:(half + 1) * S, :]
                step(nc.gpsimd.memset(km, float(DK) ** -0.5))
                step(nc.gpsimd.affine_select(out=km, in_=km, compare_op=ALU.is_ge, fill=0.0, base=0,
                                             pattern=[[-DK, HH]], channel_multiplier=1))
                step(nc.gpsimd.affine_select(out=km, in_=km, compare_op=ALU.is_ge, fill=0.0, base=DK - 1,
                                             pattern=[[DK, HH]], channel_multiplier=-1))
            step(nc.gpsimd.memset(sel[:, :, :], 0.0))
            nc.gpsimd.affine_select(out=sel[:, :, :].rearrange("e m (b h) -> e m b h", b=2),
                                    in_=sel[:, :, :].rearrange("e m (b h) -> e m b h", b=2),
                                    compare_op=ALU.not_equal, fill=1.0, base=0,
                                    pattern=[[-2, MT], [-1, 2], [0, HID]], channel_multiplier=1).then_inc(const_made, 1)
            step(nc.gpsimd.memset(ind[:, :], 0.0))
            nc.gpsimd.affine_select(out=ind[:, :].rearrange("b (c q) -> b c q", c=SEQ_T),
                                    in_=ind[:, :].rearrange("b (c q) -> b c q", c=SEQ_T),
                                    compare_op=ALU.not_equal, fill=1.0, base=0,
                                    pattern=[[-1, SEQ_T], [0, S]], channel_multiplier=1).then_inc(const_made, 1)
            nc.gpsimd.iota(iota_i[:, :], pattern=[[0, TG], [1, E]], base=0, channel_multiplier=0).then_inc(const_made, 1)
            for n in range(TG):
                step(nc.gpsimd.memset(v2[n][:, :, :, :], 0.0))
                step(nc.gpsimd.memset(v2[n][0:S, :, :, DK:VC], 1.0))
                step(nc.gpsimd.memset(v2[n][S:P, :, :, VC + DK:2 * VC], 1.0))
            def square(g, ct):
                pool.wait_ge(a_clamped, g * CT + ct + 1)
                if not first(g):
                    pool.wait_ge(h_made, (g - 1) * CT + ct + 1)
                nc.gpsimd.tensor_tensor(seqs(q_buf, ct), seqs(a_buf, ct), seqs(a_buf, ct), ALU.mult).then_inc(a2_made, 1)

            def keys(g, t):
                if not (first(g) and t < 2):
                    pool.wait_ge(score_ready, g * UNITS + 2 * (t - 1) + 1)
                nc.gpsimd.tensor_tensor(kexp[t % 2][:, :, :],
                                        cT[:, bass.ds(g * TG + t, 1), :].to_broadcast([P, HH, P]),
                                        kmask[:, :, None].to_broadcast([P, HH, P]), ALU.mult).then_inc(kexp_made, 1)

            def values2(g, t):
                if not first(g):
                    pool.wait_ge(pv_ready, (g - 1) * UNITS + 2 * t + 2 + 1)
                pool.wait_ge(kexp_made, g * TG + t + 1)
                for half in range(2):
                    rows = slice(half * S, (half + 1) * S)
                    seq = bass.ds((g * TG + t) * SEQ_T, SEQ_T)
                    src = ctx_key[rows, seq, :].rearrange("k b (n h d) -> k b n h d", h=2, d=DK)[:, :, :, half, :]
                    nc.gpsimd.tensor_tensor(v2[t][rows, :, :, half * VC:half * VC + DK], src,
                                            mask_key[rows, seq][:, :, None, None].to_broadcast([S, SEQ_T, HH, DK]),
                                            ALU.mult).then_inc(v2_made, 1)
                    pool.wait_ge(v2_made, 2 * (g * TG + t) + half + 1 + 1)
            def iteration(gA, gB, gC):
                A, Bs = gA is not None, gB is not None
                for q in range(TG):
                    if A:
                        square(gA, 2 * q)
                        square(gA, 2 * q + 1)
                    if Bs and q < 2:
                        keys(gB, q + 2)
                        values2(gB, q + 2)
                if first(gA):
                    for g in range(GROUPS):
                        pool.wait_ge(prep_copied, PREP_BIAS)
                        pool.wait_ge(prep_copied, PREP_X[g])
                        xg = x_nat[:, g * TG:(g + 1) * TG, :]
                        nc.gpsimd.tensor_tensor(xg, xg, bias_bc[:, None, 0:D].to_broadcast([P, TG, D]),
                                                ALU.add).then_inc(xb_made, 1)
                    pool.wait_ge(prep_copied, PREP_ALL)
                    pool.wait_ge(key_in, 32)
                if A:
                    for t in range(2):
                        keys(gA, t)
                        values2(gA, t)

            groups(iteration, pool)

        @block.tensor
        def _(pe):
            def prep(n):
                name, to = PREP[n], prep_bank(n)
                if n >= 4:
                    pe.wait_ge(prep_copied, n - 3)
                if name == "vec":
                    pe.wait_ge(small_in, 16 * SMALL)
                    pe.wait_ge(dve_const, 1)
                    last = nc.tensor.transpose(to[:, 0:NV], vec_rows[:, :], ident[0:NV, 0:NV])
                elif name == "mask":
                    last = nc.tensor.transpose(to[:, 0:B], mask_rows[:, :, :].rearrange("b c s -> b (c s)"), ident[0:B, 0:B])
                elif name == "wp":
                    last = nc.tensor.transpose(to[:, 0:D], wp_nat[:, :], ident[:, :])
                elif name == "rw":
                    last = nc.tensor.transpose(to[:, 0:E], rw_nat[:, :], ident[0:E, 0:E])
                elif name == "bias":
                    pe.wait_ge(dve_const, 7)
                    last = nc.tensor.matmul(to[:, 0:2 * D + E], ones_row[:, :], row_bias[:, :], start=True, stop=True)
                else:
                    src, came = (x_nat, x_in) if name[0] == "x" else (ctx_nat, ctx_in_s)
                    g = int(name[1:])
                    pe.wait_ge(came[g], 16)
                    for t in range(TG):
                        last = nc.tensor.transpose(tile(to, t), src[:, g * TG + t, :], ident[:, :])
                last.then_inc(prep_tr, 1)

            def project(g, ct):
                if first(g):
                    pe.wait_ge(waiv_in[ct // 2], 16)
                for p, (z, ready) in enumerate(((ZA, za_ready), (ZI, zi_ready), (ZV, zv_ready))):
                    if not (first(g) and ct == 0):
                        pe.wait_ge((a_made, i_made, iv_made)[p], g * CT + ct)
                    nc.tensor.matmul(z[:, :], waiv_sb[:, p, ct * P:(ct + 1) * P], xT[:, bass.ds(g * TOK, TOK)],
                                     start=True, stop=True).then_inc(ready, 1)

            def mix(gA, gC, ct):
                if ct == 0:
                    if first(gA):
                        pe.wait_ge(w_in_act, 16)
                    else:
                        pe.wait_ge(res_made[1], gA)
                    if gC is not None:
                        pe.wait_ge(hw_made, gC * MT + MT + 1)
                pe.wait_ge(h_made, gA * CT + ct + 1)
                states = h_buf[:, ct, :].rearrange("p (s k) -> p s k", k=PAD)[:, :, 1:PAD]
                last = nc.tensor.matmul(CB[:, :], wmix_sb[:, ct, :], states, start=(ct == 0), stop=(ct == CT - 1))
                if ct == CT - 1:
                    last.then_inc(mix_ready, 1)

            def turn_mix(g):
                pe.wait_ge(mixT_made, g + 1)
                for t in range(TG):
                    last = nc.tensor.transpose(tile(CB, t), tile(mixT, t), ident[:, :])
                last.then_inc(mix_turned, 1)

            def scores(g, u):
                t, half = divmod(u, 2)
                if u == 0:
                    pe.wait_ge(x1T_made, g + 1)
                if half == 0:
                    pe.wait_ge(kexp_made, g * TG + t + 1)
                if u:
                    pe.wait_ge(shifted, g * UNITS + u)
                elif not first(g):
                    pe.wait_ge(res_made[2], g)
                pe.nop(nofuse=True)
                nc.tensor.matmul(SC[:, :], ind[:, :],
                                 key_bias[:, bass.ds(g * TG + t, 1), :].to_broadcast([P, HH, S]),
                                 start=True, stop=False, skip_group_check=True)
                rows = slice(half * S, (half + 1) * S)
                for b in range(SEQ_T):
                    last = nc.tensor.matmul(SC[b * S:(b + 1) * S, :], x1T[rows, t * P + b * S:t * P + (b + 1) * S],
                                            kexp[t % 2][rows, :, b * S:(b + 1) * S],
                                            start=False, stop=True, skip_group_check=True)
                last.then_inc(score_ready, 1)

            def turn_probs(g, u):
                pe.wait_ge(exp_made, g * UNITS + u + 1)
                pe.wait_ge(pT_made, g * UNITS + u + 1)
                for p in range(PAIRS):
                    last = nc.tensor.transpose(tile(TR, p), tile(prob[u % PB], p), ident[:, :])
                last.then_inc(pT_ready, 1)

            def values(g, u):
                t, half = divmod(u, 2)
                pe.wait_ge(pT_made, g * UNITS + u + 1 + 1)
                if half == 0:
                    pe.wait_ge(v2_made, 2 * (g * TG + t + 1) + 1)
                    pe.wait_ge(attn_made, g * TG + t + 1)
                for p in range(PAIRS):
                    pair = half * PAIRS + p
                    for b in range(SEQ_T):
                        last = nc.tensor.matmul(PV[b * S:(b + 1) * S, pair * 2 * VC:(pair + 1) * 2 * VC],
                                                probT[u % 2][:, p * P + b * S:p * P + (b + 1) * S],
                                                v2[t][:, b, pair, :], start=True, stop=True)
                last.then_inc(pv_ready, 1)

            def turn(to, src):
                for t in range(TG):
                    last = nc.tensor.transpose(tile(to, t), src[:, t, :], ident[:, :])
                return last

            def turn_attn(g):
                pe.wait_ge(attn_made, g * TG + TG + 1)
                pe.wait_ge(pT_made, g * UNITS + UNITS + 1)
                turn(TR, attn).then_inc(attnT_ready, 1)

            def out_proj(g):
                pe.wait_ge(attnT_made, g + 1)
                pe.wait_ge(shifted, g * UNITS + UNITS)
                for t in range(TG):
                    nc.tensor.matmul(tile(SC, t), ones_row[:, :], row_bias[:, D:2 * D], start=True, stop=False)
                    last = nc.tensor.matmul(tile(SC, t), tile(attnT, t), wpT[:, :], start=False, stop=True)
                last.then_inc(wp_ready, 1)

            def turn_x2(g):
                pe.wait_ge(xn_made[2], g * TG + TG + 1)
                pe.wait_ge(res_made[3], g + 1)
                turn(MX, x2).then_inc(x2T_ready, 1)

            def logits(gB, g):
                pe.wait_ge(x2T_made, g + 1)
                if gB is not None:
                    pe.wait_ge(res_made[1], gB + 1)
                for t in range(TG):
                    last = nc.tensor.matmul(CB[:, t * E:(t + 1) * E], tile(x2T, t), rwT[:, :], start=True, stop=True)
                last.then_inc(lg_ready, 1)

            def hidden(g, m):
                width = P if m < MT else HID
                if m == 1:
                    pe.wait_ge(lg_made, g + 1)
                elif m >= 2:
                    pe.wait_ge(silu_made, g * (MT + 1) + m - 1 + 1)
                nc.tensor.matmul((MX, CB)[m % 2][0:width, :], w1_sb[:, m * P:m * P + width], x2T[:, :],
                                 start=True, stop=True).then_inc(hid_ready, 1)

            def turn_cf(g):
                pe.wait_ge(cf_made, g + 1)
                pe.wait_ge(silu_made, g * (MT + 1) + MT + 1)
                for t in range(TG):
                    last = nc.tensor.transpose(CB[0:E + 1, t * P:(t + 1) * P], cf[:, t, :], ident[:, :])
                last.then_inc(cfT_ready, 1)

            def spread_cf(g, m):
                if m == 0:
                    pe.wait_ge(cfT_made, g + 1)
                else:
                    pe.wait_ge(hw_made, g * MT + m + 1)
                nc.tensor.matmul(CB[:, :], sel[:, m, :], cfT[:, :], start=True, stop=True).then_inc(cb_ready, 1)

            def experts_out(g, part):
                if part == 0:
                    pe.wait_ge(silu_made, (g + 1) * (MT + 1) + 1)
                if part >= 2:
                    pe.wait_ge(hw_made, g * MT + part)
                for t in range(TG):
                    if part == 0:
                        lhsT, rhs = tile(cfT, t), b2_sb[:, :]
                    elif part == 1:
                        lhsT, rhs = tile(hs[0:HID, MT, :], t), w2_sb[0:HID, MT, :]
                    else:
                        lhsT, rhs = tile(hw[:, part - 2, :], t), w2_sb[:, part - 2, :]
                    last = nc.tensor.matmul(tile(MX, t), lhsT, rhs, start=(part == 0 and t == 0),
                                            stop=(part == MT + 1), skip_group_check=True)
                if part == MT + 1:
                    last.then_inc(y_ready, 1)

            def turn_x1(g):
                pe.wait_ge(xn_made[1], g * TG + TG + 1)
                if first(g):
                    pe.wait_ge(prep_copied, PREP_ALL)
                else:
                    pe.wait_ge(attnT_made, g)
                turn(TR, x1).then_inc(x1T_ready, 1)

            def iteration(gA, gB, gC):
                A, Bs, C = gA is not None, gB is not None, gC is not None
                if A:
                    project(gA, 0)
                if Bs:
                    mix(gB, None, 6)
                    mix(gB, None, 7)
                if A:
                    project(gA, 1)
                if Bs:
                    turn_mix(gB)
                if C:
                    turn_x2(gC)
                    logits(gB, gC)
                    hidden(gC, 0)
                if Bs:
                    turn_x1(gB)
                if A:
                    project(gA, 2)
                if Bs:
                    scores(gB, 0)
                if A:
                    project(gA, 3)
                if Bs:
                    scores(gB, 1)
                if A:
                    project(gA, 4)
                if Bs:
                    scores(gB, 2)
                if C:
                    hidden(gC, 1)
                if Bs:
                    scores(gB, 3)
                if A:
                    project(gA, 5)
                if Bs:
                    turn_probs(gB, 0)
                    scores(gB, 4)
                    values(gB, 0)
                    turn_probs(gB, 1)
                    scores(gB, 5)
                    values(gB, 1)
                    turn_probs(gB, 2)
                if A:
                    project(gA, 6)
                if Bs:
                    turn_probs(gB, 3)
                    values(gB, 2)
                    scores(gB, 6)
                if A:
                    project(gA, 7)
                if Bs:
                    values(gB, 3)
                if C:
                    hidden(gC, 2)
                    hidden(gC, 3)
                if Bs:
                    scores(gB, 7)
                if C:
                    hidden(gC, 4)
                    turn_cf(gC)
                if first(gA):
                    for n in range(EARLY, len(PREP)):
                        prep(n)
                    pe.wait_ge(w_in, 16 * 6)
                    pe.wait_ge(const_made, 3)
                    pe.wait_ge(kb_made, 2)
                    pe.wait_ge(dve_const, DVE_CONSTS)
                if C:
                    spread_cf(gC, 0)
                    experts_out(gC, 0)
                if Bs:
                    turn_probs(gB, 4)
                if C:
                    spread_cf(gC, 1)
                if Bs:
                    turn_probs(gB, 5)
                    values(gB, 4)
                if C:
                    experts_out(gC, 1)
                if Bs:
                    turn_probs(gB, 6)
                    values(gB, 5)
                    turn_probs(gB, 7)
                    values(gB, 6)
                if C:
                    spread_cf(gC, 2)
                    experts_out(gC, 2)
                if Bs:
                    values(gB, 7)
                if C:
                    spread_cf(gC, 3)
                    experts_out(gC, 3)
                if Bs:
                    turn_attn(gB)
                if C:
                    experts_out(gC, 4)
                if A:
                    mix(gA, gC, 0)
                if Bs:
                    out_proj(gB)
                if C:
                    experts_out(gC, 5)
                if A:
                    mix(gA, gC, 1)
                    mix(gA, gC, 2)
                    mix(gA, gC, 3)
                    mix(gA, gC, 4)
                    mix(gA, gC, 5)

            head_start(pe, score_ready, pT_ready, pv_ready, attnT_ready, x1T_ready)
            pe.wait_ge(ident_made, 1)
            pe.wait_ge(small_in, 16 * SMALL)
            for n in range(EARLY):
                prep(n)
            pe.wait_ge(prep_copied, EARLY)
            groups(iteration, pe)

        @block.scalar
        def _(act):
            head_start(act, silu_made, pT_made, dev_made[1], dev_made[2], dev_made[3])
            row = lambda v: v.rearrange("(a n) -> a n", a=1)
            act.wait_ge(dve_const, 2)
            act.dma_start(vec_rows[0:CT, :], decay_bias.rearrange("(c p) -> c p", p=P)).then_inc(small_in, 16)
            act.dma_start(vec_rows[R_B1:R_B1 + MT, :], r_b1.rearrange("(m e) h -> m (e h)", e=2)).then_inc(small_in, 16)
            act.dma_start(vec_rows[R_B1 + MT:R_B1 + MT + 1, 0:HID], row(s_b1)).then_inc(small_in, 16)
            act.dma_start(vec_rows[R_MASK:NV, :], mask.rearrange("(t b) s -> t (b s)", b=SEQ_T)).then_inc(small_in, 16)
            for c in range(SEQ_T):
                act.dma_start(mask_rows[:, c, :], mask).then_inc(small_in, 16)
            act.dma_start(mask_pair[:, :, :], mask.rearrange("(t b) s -> b t s", b=SEQ_T)).then_inc(small_in, 16)
            act.dma_start(row_bias[0:1, 0:D], row(b_mix)).then_inc(small_in, 16)
            act.dma_start(row_bias[0:1, D:2 * D], row(bp)).then_inc(small_in, 16)
            act.dma_start(row_bias[0:1, 2 * D:], row(expert_bias)).then_inc(small_in, 16)
            act.dma_start(wp_nat[:, :], wp).then_inc(small_in, 16)
            act.dma_start(rw_nat[:, :], routing_w).then_inc(small_in, 16)
            act.dma_start(wmix_sb[:, :, :], w_mix.rearrange("(c p) d -> p c d", p=P)).then_inc(w_in_act, 16)

            def prep_copy(n):
                name, src = PREP[n], prep_bank(n)
                dst = {"vec": vec[:, :], "mask": mask_key[:, :], "wp": wpT[:, :], "rw": rwT[:, :], "bias": bias_bc[:, :]}.get(name)
                if dst is None:
                    g = int(name[1:])
                    dst = xT[:, g * TOK:(g + 1) * TOK] if name[0] == "x" else flat(cT[:, g * TG:(g + 1) * TG, :])
                act.wait_ge(prep_tr, n + 1)
                nc.scalar.activation(dst, src[:, 0:dst.shape[1]], ACT.Copy).then_inc(prep_copied, 1)

            def gates(g, ct):
                act.wait_ge(za_ready, g * CT + ct + 1)
                if not first(g):
                    act.wait_ge(h_made, (g - 1) * CT + ct + 1)
                nc.scalar.activation(seqs(a_buf, ct), toks(ZA[:, :]), ACT.Sigmoid, bias=vec[:, ct:ct + 1]).then_inc(a_made, 1)
                act.wait_ge(zi_ready, g * CT + ct + 1)
                if not first(g):
                    act.wait_ge(sig_made, (g - 1) * CT + ct + 1)
                nc.scalar.activation(iv_buf[:, ct, :], ZI[:, :], ACT.Sigmoid).then_inc(i_made, 1)

            def gate_sqrt(g, ct):
                act.wait_ge(a2_made, g * CT + ct + 1)
                nc.scalar.activation(seqs(q_buf, ct), seqs(q_buf, ct), ACT.Sqrt, bias=1.0, scale=-1.0).then_inc(s_made, 1)

            def exps(g, u):
                act.wait_ge(shifted, g * UNITS + u + 1)
                nc.scalar.activation(prob[u % PB][:, :], prob[u % PB][:, :], ACT.Exp).then_inc(exp_made, 1)

            def probs_turned(g, u):
                act.wait_ge(pT_ready, g * UNITS + u + 1 + 1)
                act.wait_ge(pv_ready, g * UNITS + max(0, u - 1) + 1)
                nc.scalar.activation(probT[u % 2][:, :], TR[:, :], ACT.Copy).then_inc(pT_made, 1)

            def deviation(n, g):
                act.wait_ge(mv_made[n], g * TG + TG)
                act.wait_ge(rstd_made[n], g + 1)
                nc.scalar.activation(norm_sb[n][2][:, :], norm_sb[n][1][:, :, 1], ACT.Sqrt,
                                     bias=eps_col[:, :]).then_inc(dev_made[n], 1)

            def mix_copied(g):
                act.wait_ge(mix_ready, g + 1)
                act.wait_ge(score_ready, g * UNITS + 1)
                nc.scalar.activation(mixT[:, :], CB[:, :], ACT.Copy).then_inc(mixT_made, 1)

            def x1_copied(g):
                act.wait_ge(x1T_ready, g + 2)
                nc.scalar.activation(x1T[:, :], TR[:, :], ACT.Copy).then_inc(x1T_made, 1)

            def attn_copied(g):
                act.wait_ge(attnT_ready, g + 2)
                nc.scalar.activation(attnT[:, :], TR[:, :], ACT.Copy).then_inc(attnT_made, 1)

            def x2_copied(g):
                act.wait_ge(x2T_ready, g + 1)
                nc.scalar.activation(x2T[:, :], MX[:, :], ACT.Copy).then_inc(x2T_made, 1)

            def route_exp(g):
                act.wait_ge(nabs_made, g + 1)
                nc.scalar.activation(rt[1][:, :, :], rt[0][:, :, :], ACT.Exp).then_inc(expl_made, 1)

            def route_ln(g):
                act.wait_ge(route_step, g * ROUTE + 1)
                nc.scalar.activation(rt[3][:, :, :], rt[2][:, :, :], ACT.Ln).then_inc(ln1p_made, 1)

            def route_sqrt(g):
                act.wait_ge(sp_made, g + 1)
                nc.scalar.activation(rt[9][:, :, :], rt[8][:, :, :], ACT.Sqrt).then_inc(act_made, 1)

            def combine_copied(g):
                act.wait_ge(cfT_ready, g + 1)
                nc.scalar.activation(cfT[0:E + 1, :], CB[0:E + 1, :], ACT.Copy).then_inc(cfT_made, 1)

            def iteration(gA, gB, gC):
                A, Bs, C = gA is not None, gB is not None, gC is not None
                if A:
                    gates(gA, 0)
                if Bs:
                    mix_copied(gB)
                if C:
                    x2_copied(gC)
                if Bs:
                    deviation(1, gB)
                if A:
                    gates(gA, 1)
                if Bs:
                    x1_copied(gB)
                if A:
                    gates(gA, 2)
                    gates(gA, 3)
                    gates(gA, 4)
                if Bs:
                    nc.scalar.preload_act_table_set("natural_log_exp_and_others")
                if C:
                    nc.scalar.preload_act_table_set("natural_log_exp_and_others")
                    route_exp(gC)
                if Bs:
                    exps(gB, 0)
                    exps(gB, 1)
                    exps(gB, 2)
                    exps(gB, 3)
                if C:
                    route_ln(gC)
                if Bs:
                    probs_turned(gB, 0)
                if A:
                    gate_sqrt(gA, 0)
                    gate_sqrt(gA, 1)
                if Bs:
                    probs_turned(gB, 1)
                if A:
                    gate_sqrt(gA, 2)
                    gate_sqrt(gA, 3)
                if C:
                    route_sqrt(gC)
                if A:
                    gates(gA, 5)
                if Bs:
                    probs_turned(gB, 2)
                if A:
                    gates(gA, 6)
                if Bs:
                    probs_turned(gB, 3)
                if A:
                    gates(gA, 7)
                if C:
                    silu(gC, 0)
                    silu(gC, 1)
                    silu(gC, 2)
                    silu(gC, 3)
                    silu(gC, 4)
                    combine_copied(gC)
                if Bs:
                    nc.scalar.preload_act_table_set("natural_log_exp_and_others")
                    exps(gB, 4)
                    exps(gB, 5)
                    exps(gB, 6)
                    exps(gB, 7)
                    probs_turned(gB, 4)
                if A:
                    gate_sqrt(gA, 4)
                if Bs:
                    probs_turned(gB, 5)
                if A:
                    gate_sqrt(gA, 5)
                if Bs:
                    probs_turned(gB, 6)
                if A:
                    gate_sqrt(gA, 6)
                if Bs:
                    probs_turned(gB, 7)
                if A:
                    gate_sqrt(gA, 7)
                if first(gA):
                    for n in range(EARLY, len(PREP)):
                        prep_copy(n)
                if Bs:
                    attn_copied(gB)
                    deviation(2, gB)
                if C:
                    deviation(3, gC)

            def silu(g, m):
                width = P if m < MT else HID
                act.wait_ge(hid_ready, g * (MT + 1) + m + 1)
                nc.scalar.activation(hs[0:width, m, :], (MX, CB)[m % 2][0:width, :], ACT.Silu,
                                     bias=vec[0:width, R_B1 + m:R_B1 + m + 1]).then_inc(silu_made, 1)

            for n in range(EARLY):
                prep_copy(n)
            act.wait_ge(prep_copied, EARLY)
            act.wait_ge(dve_const, DVE_CONSTS)
            groups(iteration, act)

        @block.vector
        def _(dve):
            head_start(dve, attn_made, hw_made, res_made[3], rstd_made[1], rstd_made[2], rstd_made[3], xn_made[1], xn_made[2], xn_made[3])
            nc.vector.memset(vec_rows[:, :], 0.0).then_inc(dve_const, 1)
            nc.vector.memset(row_bias[:, :], 0.0).then_inc(dve_const, 1)
            nc.vector.memset(ones_row[:, :], 0.0).then_inc(dve_const, 1)
            nc.vector.memset(b2_sb[:, :], 0.0).then_inc(dve_const, 1)
            nc.vector.memset(key_bias[:, :, :], 0.0).then_inc(dve_const, 1)
            nc.vector.memset(cfT[:, :], 0.0).then_inc(dve_const, 1)
            dve.wait_ge(dve_const, 3)
            nc.vector.memset(ones_row[0:1, :], 1.0).then_inc(dve_const, 1)
            nc.vector.memset(eps_col[:, :], EPS).then_inc(dve_const, 1)
            nc.vector.memset(cf[:, :, E:], 1.0).then_inc(dve_const, 1)
            pads = lambda buf: buf.rearrange("p (s k) -> p s k", k=PAD)[:, :, 0]
            nc.vector.memset(restart[:, :], 0.0).then_inc(dve_const, 1)
            nc.vector.memset(a_buf[:, :, :].rearrange("p c (s k) -> p (c s) k", k=PAD)[:, :, 0], 0.0).then_inc(dve_const, 1)
            nc.vector.memset(q_buf[:, :, :].rearrange("p c (s k) -> p (c s) k", k=PAD)[:, :, 0], 0.0).then_inc(dve_const, 1)
            dve.wait_ge(dve_const, 10)
            nc.vector.memset(pads(restart[:, :]), GSTART).then_inc(dve_const, 1)
            dve.wait_ge(small_in, 16 * SMALL)
            nc.vector.tensor_scalar(key_bias[0:SEQ_T, :, :], mask_pair[:, :, :], 0.0, NEG, ALU.is_equal, ALU.mult).then_inc(kb_made, 1)
            dve.wait_ge(const_made, 3)
            nc.vector.tensor_copy(flat(iota_f[:, :, :]), iota_i[:, :]).then_inc(kb_made, 1)
            dve.wait_ge(dve_const, DVE_CONSTS)
            dve.wait_ge(kb_made, 2)

            def clamp_gate(g, ct):
                dve.wait_ge(a_made, g * CT + ct + 1)
                nc.vector.tensor_scalar(seqs(a_buf, ct), seqs(a_buf, ct), TINY, 1.0, ALU.max, ALU.min).then_inc(a_clamped, 1)
                dve.wait_ge(i_made, g * CT + ct + 1)
                dve.wait_ge(zv_ready, g * CT + ct + 1)
                nc.vector.tensor_tensor(iv_buf[:, ct, :], ZV[:, :], iv_buf[:, ct, :], ALU.mult).then_inc(iv_made, 1)

            def scan_decay(g, ct):
                dve.wait_ge(a_clamped, g * CT + ct + 1)
                if not first(g) and ct == 0:
                    dve.wait_ge(mix_ready, g)
                nc.vector.tensor_tensor_scan(h_buf[:, ct, :], a_buf[:, ct, :], restart[:, :], 0.0,
                                             ALU.mult, ALU.add).then_inc(g_made, 1)

            def scan_state(g, ct):
                at = g * CT + ct + 1
                dve.wait_ge(s_made, at)
                dve.wait_ge(iv_made, at)
                nc.vector.scalar_tensor_tensor(seqs(q_buf, ct), seqs(q_buf, ct), CLAMP, toks(iv_buf[:, ct, :]),
                                               ALU.max, ALU.mult).then_inc(sig_made, 1)
                dve.wait_ge(sig_made, at)
                dve.wait_ge(g_made, at)
                nc.vector.scalar_tensor_tensor(q_buf[:, ct, :], h_buf[:, ct, :], 1.0, q_buf[:, ct, :],
                                               ALU.min, ALU.mult).then_inc(u_made, 1)
                dve.wait_ge(u_made, at)
                nc.vector.tensor_tensor_scan(h_buf[:, ct, :], a_buf[:, ct, :], q_buf[:, ct, :], 0.0,
                                             ALU.mult, ALU.add).then_inc(h_made, 1)

            def shift(g, u):
                s3 = lambda a: a.rearrange("p (h k) -> p h k", k=S)
                dve.wait_ge(score_ready, g * UNITS + u + 1 + 1)
                nc.vector.tensor_reduce(smax[:, u % 2, :], s3(SC[:, :]), AXX, ALU.max).then_inc(max_made, 1)
                dve.wait_ge(max_made, g * UNITS + u + 1)
                dve.wait_ge(pT_ready, g * UNITS + max(0, u - PB + 1) + 1)
                nc.vector.tensor_tensor(s3(prob[u % PB][:, :]), s3(SC[:, :]),
                                        smax[:, u % 2, :].unsqueeze(2).to_broadcast([P, HH, S]),
                                        ALU.subtract).then_inc(shifted, 1)

            def attend(g, t):
                pv = PV[:, 0:NH * VC].rearrange("p (h c) -> p h c", c=VC)
                dve.wait_ge(pv_ready, g * UNITS + 2 * t + 2 + 1)
                nc.vector.reciprocal(rden[:, t % 2, :], pv[:, :, DK]).then_inc(rden_made, 1)
                dve.wait_ge(rden_made, g * TG + t + 1)
                dve.wait_ge(maskq_made, g + 1)
                nc.vector.tensor_scalar(rdenm[:, t % 2, :], rden[:, t % 2, :], mask_q[:, t:t + 1], None,
                                        ALU.mult).then_inc(rdenm_made, 1)
                dve.wait_ge(rdenm_made, g * TG + t + 1)
                if t == 0:
                    dve.wait_ge(attnT_ready, g + 1)
                nc.vector.tensor_tensor(attn[:, t, :].rearrange("p (h c) -> p h c", c=DK), pv[:, :, 0:DK],
                                        rdenm[:, t % 2, :].unsqueeze(2).to_broadcast([P, NH, DK]),
                                        ALU.mult).then_inc(attn_made, 1)

            def stats(n, g, r):
                st, mv, ln, rs = norm_sb[n]
                dve.wait_ge(res_made[n], g + (2 if n == 3 else 1))
                for t in range(TG):
                    nc.vector.bn_stats(st[:, t, :], r[:, t, :]).then_inc(st_made[n], 1)
                dve.wait_ge(dev_made[n], g + 1)
                for t in range(TG):
                    dve.wait_ge(st_made[n], g * TG + t + 1)
                    dve.nop(nofuse=True)
                    nc.vector.bn_aggr(mv[:, t, :], st[:, t, :]).then_inc(mv_made[n], 1)

            def normalise(n, g, r, xn):
                st, mv, ln, rs = norm_sb[n]
                dve.wait_ge(dev_made[n], g + 2)
                nc.vector.reciprocal(rs[:, :], ln[:, :]).then_inc(rstd_made[n], 1)
                dve.wait_ge(rstd_made[n], g + 2)
                for t in range(TG):
                    nc.vector.tensor_scalar(xn[:, t, :], r[:, t, :], mv[:, t, 0:1], rs[:, t:t + 1],
                                            ALU.subtract, ALU.mult).then_inc(xn_made[n], 1)

            def residual1(g):
                dve.wait_ge(mix_turned, g + 1)
                dve.wait_ge(x1T_ready, g + 1)
                dve.wait_ge(xb_made, g + 1)
                nc.vector.tensor_tensor(flat(r1[:, :, :]), CB[:, :],
                                        x_nat[:, bass.ds(g * TG, TG), :].rearrange("p t d -> p (t d)"),
                                        ALU.add).then_inc(res_made[1], 1)
                stats(1, g, r1)

            def norm1(g):
                normalise(1, g, r1, x1)

            def residual2(g):
                dve.wait_ge(wp_ready, g + 1)
                if not first(g):
                    dve.wait_ge(x2T_ready, g)
                for t in range(TG):
                    last = nc.vector.scalar_tensor_tensor(r2[:, t, :], tile(SC, t), mask_q[:, t:t + 1], x1[:, t, :],
                                                          ALU.mult, ALU.add)
                last.then_inc(res_made[2], 1)
                stats(2, g, r2)

            def route_logits(g):
                dve.wait_ge(lg_ready, g + 1)
                nc.vector.tensor_tensor(lg[:, :, :], CB[:, 0:TG * E].rearrange("p (t e) -> p t e", e=E),
                                        bias_bc[:, None, 2 * D:].to_broadcast([P, TG, E]), ALU.add).then_inc(lg_made, 1)
                dve.wait_ge(lg_made, g + 1)
                nc.vector.scalar_tensor_tensor(rt[0][:, :, :], lg[:, :, :], -1.0, lg[:, :, :], ALU.mult, ALU.min).then_inc(nabs_made, 1)
                for t in range(TG):
                    nc.vector.max(top[:, t, :], lg[:, t, :]).then_inc(top_made, 1)
                for t in range(TG):
                    dve.wait_ge(top_made, g * TG + t + 1)
                    dve.nop(nofuse=True)
                    nc.vector.max_index(top_i[:, t, :], top[:, t, :], lg[:, t, :]).then_inc(topi_made, 1)
                dve.wait_ge(topi_made, g * TG + TG)
                nc.vector.tensor_copy(top_f[:, :, :], top_i[:, :, :]).then_inc(topf_made, 1)

            e, u, dlt, dg, rc = rt[1], rt[2], rt[4], rt[5], rt[6]

            def route_log(g):
                step = lambda n: dve.wait_ge(route_step, g * ROUTE + n)
                dve.wait_ge(expl_made, g + 1)
                nc.vector.tensor_scalar(u[:, :, :], e[:, :, :], 1.0, None, ALU.add).then_inc(route_step, 1)
                step(1)
                nc.vector.tensor_scalar(dlt[:, :, :], u[:, :, :], 1.0, None, ALU.subtract).then_inc(route_step, 1)
                nc.vector.tensor_scalar(rt[11][:, :, :], u[:, :, :], 1.0, None, ALU.is_equal).then_inc(route_step, 1)
                step(2)
                nc.vector.tensor_scalar(dg[:, :, :], dlt[:, :, :], 1e-30, None, ALU.max).then_inc(route_step, 1)
                step(4)
                nc.vector.reciprocal(rc[:, :, :], dg[:, :, :]).then_inc(route_step, 1)
                dve.wait_ge(topf_made, g + 1)
                pick = lambda n: top_f[:, :, n:n + 1].to_broadcast([P, TG, E])
                nc.vector.tensor_tensor(rt[10][:, :, :], iota_f[:, :, :], pick(0), ALU.is_equal).then_inc(pick_step, 1)
                nc.vector.tensor_tensor(rt[7][:, :, :], iota_f[:, :, :], pick(1), ALU.is_equal).then_inc(pick_step, 1)
                dve.wait_ge(pick_step, g * PICK + 2)
                nc.vector.tensor_tensor(rt[10][:, :, :], rt[10][:, :, :], rt[7][:, :, :], ALU.add).then_inc(pick_step, 1)

            def route_softplus(g):
                dve.wait_ge(ln1p_made, g + 1)
                dve.wait_ge(route_step, g * ROUTE + 5)
                nc.vector.tensor_tensor(rt[3][:, :, :], rt[3][:, :, :], rc[:, :, :], ALU.mult).then_inc(pick_step, 1)
                dve.wait_ge(pick_step, g * PICK + 4)
                nc.vector.tensor_tensor(rt[3][:, :, :], rt[3][:, :, :], rt[11][:, :, :], ALU.add).then_inc(pick_step, 1)
                dve.wait_ge(pick_step, g * PICK + 5)
                nc.vector.tensor_tensor(rt[3][:, :, :], rt[3][:, :, :], e[:, :, :], ALU.mult).then_inc(pick_step, 1)
                dve.wait_ge(pick_step, g * PICK + 6)
                nc.vector.scalar_tensor_tensor(rt[8][:, :, :], lg[:, :, :], 0.0, rt[3][:, :, :], ALU.max, ALU.add).then_inc(sp_made, 1)

            def route_combine(g):
                dve.wait_ge(act_made, g + 1)
                nc.vector.tensor_tensor(cf[:, :, 0:E], rt[9][:, :, :], rt[10][:, :, :], ALU.mult).then_inc(cf_made, 1)

            def weigh(g, m):
                dve.wait_ge(cb_ready, g * MT + m + 1)
                dve.wait_ge(silu_made, g * (MT + 1) + m + 1 + 1)
                nc.vector.tensor_tensor(hw[:, m, :], CB[:, :], hs[:, m, :], ALU.mult).then_inc(hw_made, 1)

            def residual3(g):
                dve.wait_ge(y_ready, g + 1)
                dve.wait_ge(out_done, 16 * g + 16)
                nc.vector.tensor_tensor(flat(r3[:, :, :]), MX[:, :], flat(x2[:, :, :]), ALU.add).then_inc(res_made[3], 1)
                stats(3, g, r3)

            def norm3(g):
                normalise(3, g, r3, y_out)

            def query_mask(g):
                dve.wait_ge(prep_copied, PREP_ALL)
                nc.vector.tensor_copy(mask_q[:, :], vec[:, bass.ds(R_MASK + g * TG, TG)]).then_inc(maskq_made, 1)

            def iteration(gA, gB, gC):
                A, Bs, C = gA is not None, gB is not None, gC is not None
                if C:
                    normalise(2, gC, r2, x2)
                if A:
                    clamp_gate(gA, 0)
                if Bs:
                    residual1(gB)
                if A:
                    clamp_gate(gA, 1)
                if Bs:
                    norm1(gB)
                    query_mask(gB)
                if C:
                    route_logits(gC)
                if A:
                    clamp_gate(gA, 2)
                    scan_decay(gA, 0)
                    scan_decay(gA, 1)
                if Bs:
                    shift(gB, 0)
                if A:
                    clamp_gate(gA, 3)
                    scan_decay(gA, 2)
                if Bs:
                    shift(gB, 1)
                if A:
                    clamp_gate(gA, 4)
                    scan_decay(gA, 3)
                if Bs:
                    shift(gB, 2)
                if C:
                    route_log(gC)
                if Bs:
                    shift(gB, 3)
                if A:
                    scan_decay(gA, 4)
                if C:
                    route_softplus(gC)
                if Bs:
                    shift(gB, 4)
                if A:
                    scan_state(gA, 0)
                if Bs:
                    shift(gB, 5)
                if A:
                    scan_state(gA, 1)
                    clamp_gate(gA, 5)
                if Bs:
                    attend(gB, 0)
                if A:
                    scan_decay(gA, 5)
                    clamp_gate(gA, 6)
                if C:
                    route_combine(gC)
                if Bs:
                    shift(gB, 6)
                if A:
                    scan_state(gA, 2)
                    scan_decay(gA, 6)
                if Bs:
                    attend(gB, 1)
                    shift(gB, 7)
                if A:
                    clamp_gate(gA, 7)
                    scan_decay(gA, 7)
                    scan_state(gA, 3)
                if C:
                    weigh(gC, 0)
                    weigh(gC, 1)
                if Bs:
                    attend(gB, 2)
                if A:
                    scan_state(gA, 4)
                if C:
                    weigh(gC, 2)
                if Bs:
                    attend(gB, 3)
                if C:
                    weigh(gC, 3)
                if A:
                    scan_state(gA, 5)
                if Bs:
                    residual2(gB)
                if A:
                    scan_state(gA, 6)
                if C:
                    residual3(gC)
                if A:
                    scan_state(gA, 7)
                if C:
                    norm3(gC)

            groups(iteration, dve)


_INS = ['x', 'ctx_1024', 'mask_BxS2_fk1', 'L0_attn_W_aiv', 'L0_attn_decay_bias', 'L0_attn_W_mix',
        'L0_attn_b_mix', 'L0_xattn_Wp', 'L0_xattn_bp', 'L0_ffn_routing_W', 'L0_ffn_expert_bias',
        'L0_ffn_sW1', 'L0_ffn_sb1', 'L0_ffn_sW2', 'L0_ffn_sb2', 'L0_ffn_rW1', 'L0_ffn_rb1',
        'L0_ffn_rW2', 'L0_ffn_rb2']
_OUTS = [((32, 64, 128), 'float32')]


def kernel(**inputs):
    import numpy as _np
    import concourse.bacc as _bacc
    from concourse import mybir as _mybir
    from concourse.bass_utils import run_bass_kernel_spmd as _run

    nc = _bacc.Bacc("TRN2", target_bir_lowering=False, num_devices=1)
    arrays, args = {}, []
    for name in _INS:
        a = _np.ascontiguousarray(inputs[name])
        arrays[f"in_{name}_dram"] = a
        args.append(nc.dram_tensor(f"in_{name}_dram", a.shape, _mybir.dt.from_np(a.dtype), kind="ExternalInput").ap())
    for i, (shape, dtype) in enumerate(_OUTS):
        dt = _mybir.dt.from_np(_np.dtype(dtype))
        args.append(nc.dram_tensor(f"out_{i}_dram", shape, dt, kind="ExternalOutput").ap())
    decoder_layer(nc, *args)
    r = _run(nc, [arrays], core_ids=[0])
    return r.results[0]["out_0_dram"]
```

```python
import concourse.bass as bass
from concourse import mybir
from contextlib import ExitStack


def decoder_layer(nc, x, ctx_in, mask, w_aiv, decay_bias, w_mix, b_mix, wp, bp, routing_w,
                  expert_bias, s_w1, s_b1, s_w2, s_b2, r_w1, r_b1, r_w2, r_b2, out):
    F32, BF16, U32 = mybir.dt.float32, mybir.dt.bfloat16, mybir.dt.uint32
    ALU, ACT, AXX = mybir.AluOpType, mybir.ActivationFunctionType, mybir.AxisListType.X

    B, S, D = x.shape
    P = 128
    SEQ_T = P // S
    TILES = B * S // P
    TG = 4
    GROUPS = TILES // TG
    TOK = TG * P
    SEQ_G = TG * SEQ_T
    REC = w_mix.shape[0]
    CT = REC // P
    PAD = S + 1
    LEN = SEQ_G * PAD
    NH = 16
    DK = D // NH
    HH = NH // 2
    PAIRS = HH // 2
    UNITS = 2 * TG
    VC = DK + 1
    E, HID = r_b1.shape
    MT = E * HID // P
    EPS, TINY, CLAMP = 1e-5, 1e-10, 1e-4
    GSTART = 1.0 / TINY
    NEG = -1e9

    with ExitStack() as stack:
        def sb(name, shape, dt=F32):
            return stack.enter_context(nc.sbuf_tensor(name, shape, dt))

        def sem(name):
            return stack.enter_context(nc.semaphore(name))

        x_nat = sb("x_nat", [P, TILES, D])
        ctx_nat = sb("ctx_nat", [P, TILES, D])
        ctx_key = sb("ctx_key", [P, B, D])
        waiv_sb = sb("waiv_sb", [P, 3, REC])
        wmix_sb = sb("wmix_sb", [P, CT, D])
        w1_sb = sb("w1_sb", [P, (E + 1) * HID])
        w2_sb = sb("w2_sb", [P, MT + 1, D])
        PART = 3
        ROWS = (E + 1) * PART * PART
        b2_rows = sb("b2_rows", [ROWS, D])
        b2_part = [sb(f"b2_part{n}", [ROWS, D], BF16) for n in range(PART)]
        b2_bf = sb("b2_bf", [ROWS, D], BF16)
        part_one = sb("part_one", [ROWS, PART, ROWS // PART])
        part_of = sb("part_of", [ROWS, PART])
        wp_nat = sb("wp_nat", [P, D])
        wpT = sb("wpT", [P, D])
        rw_nat = sb("rw_nat", [E, D])
        rwT = sb("rwT", [P, E])
        NV = CT + MT + 1 + TILES
        R_B1, R_MASK = CT, CT + MT + 1
        vec_rows = sb("vec_rows", [NV, P])
        vec = sb("vec", [P, NV])
        mask_rows = sb("mask_rows", [B, SEQ_T, S])
        mask_key = sb("mask_key", [P, B])
        mask_pair = sb("mask_pair", [SEQ_T, TILES, S])
        key_bias = sb("key_bias", [P, TILES, S], BF16)
        bp_rows = sb("bp_rows", [ROWS, D])
        bp_bf = sb("bp_bf", [ROWS, D], BF16)
        three = sb("three", [ROWS, P], BF16)
        row_bias = sb("row_bias", [P, D + E])
        bias_bc = sb("bias_bc", [P, D + E])
        ones_row = sb("ones_row", [P, P])
        ident = sb("ident", [P, P])
        kmask = sb("kmask", [P, HH])
        sel = sb("sel", [ROWS, MT, P], BF16)
        ident_bf = sb("ident_bf", [P, P], BF16)
        ind = sb("ind", [P, P], BF16)
        iota_i = sb("iota_i", [P, TG * E], mybir.dt.int32)
        iota_f = sb("iota_f", [P, TG, E])
        restart = sb("restart", [P, LEN])

        xT = sb("xT", [P, TILES * P])
        cT = sb("cT", [P, TILES, P])
        a_buf = sb("a_buf", [P, CT, LEN])
        q_buf = sb("q_buf", [P, CT, LEN])
        h_buf = sb("h_buf", [P, CT, LEN])
        iv_buf = sb("iv_buf", [P, CT, TOK])
        r1 = sb("r1", [P, TG, D])
        x1 = r1
        x1T = sb("x1T", [P, TOK])
        mixT = x1T

        kexp = [sb(f"kexp{n}", [P, HH, P]) for n in range(2)]
        v2 = [sb(f"v2{n}", [P, SEQ_T, HH, 2 * VC]) for n in range(TG)]
        PB = 4
        prob = [sb(f"prob{n}", [P, HH * S]) for n in range(PB)]
        probT = [sb(f"probT{n}", [P, HH * S]) for n in range(2)]
        smax = sb("smax", [P, 2, HH])
        mask_q = sb("mask_q", [P, TG])
        rden = sb("rden", [P, 2, NH])
        rdenm = sb("rdenm", [P, 2, NH])
        attn = sb("attn", [P, TG, D])
        attnT = sb("attnT", [P, TOK])
        r2 = sb("r2", [P, TG, D])
        x2 = sb("x2", [P, TG, D])
        x2T = sb("x2T", [P, TOK])
        lg = sb("lg", [P, TG, E])
        top = sb("top", [P, TG, 8])
        top_i = sb("top_i", [P, TG, 8], U32)
        top_f = sb("top_f", [P, TG, 8])
        rt = [sb(f"rt{n}", [P, TG, E]) for n in range(12)]
        cf = sb("cf", [P, TG, E])
        cf_rest = sb("cf_rest", [P, TG, E])
        cf_part = sb("cf_part", [P, TG, ROWS], BF16)
        cfT = sb("cfT", [ROWS, TOK], BF16)
        hs = sb("hs", [P, MT + 1, TOK])
        hw = ctx_nat[:, :, :].rearrange("p (m t) d -> p m (t d)", m=MT)
        r3 = sb("r3", [P, TG, D])
        y_out = r3
        norm_sb = {n: (sb(f"st{n}", [P, TG, 6]), sb(f"mv{n}", [P, TG, 2]),
                       sb(f"ln{n}", [P, TG]), sb(f"rstd{n}", [P, TG])) for n in (1, 2, 3)}

        bank = [stack.enter_context(nc.psum_tensor(f"bank{n}", [P, 512], F32)) for n in range(8)]
        ZA, ZI, ZV, SC, TR, PV, CB, MX = bank

        x_in = [sem(f"x_in{g}") for g in range(GROUPS)]
        ctx_in_s = [sem(f"ctx_in{g}") for g in range(GROUPS)]
        key_in = sem("key_in")
        waiv_in = [sem(f"waiv_in{n}") for n in range(4)]
        vec_in, small_in = sem("vec_in"), sem("small_in")
        w_in = sem("w_in")
        out_done = sem("out_done")
        ident_made = sem("ident_made")
        const_made = sem("const_made")
        pool_step = sem("pool_step")
        dve_const = sem("dve_const")
        prep_tr = sem("prep_tr")
        prep_copied = sem("prep_copied")
        xb_made = sem("xb_made")
        za_ready, zi_ready, zv_ready = sem("za_ready"), sem("zi_ready"), sem("zv_ready")
        a_made, i_made, a2_made, s_made = sem("a_made"), sem("i_made"), sem("a2_made"), sem("s_made")
        a_clamped, iv_made, g_made = sem("a_clamped"), sem("iv_made"), sem("g_made")
        sig_made, u_made, h_made = sem("sig_made"), sem("u_made"), sem("h_made")
        mix_ready, mixT_made, mix_turned = sem("mix_ready"), sem("mixT_made"), sem("mix_turned")
        res_made = {n: sem(f"res_made{n}") for n in (1, 2, 3)}
        st_made = {n: sem(f"st_made{n}") for n in (1, 2, 3)}
        mv_made = {n: sem(f"mv_made{n}") for n in (1, 2, 3)}
        dev_made = {n: sem(f"dev_made{n}") for n in (1, 2, 3)}
        rstd_made = {n: sem(f"rstd_made{n}") for n in (1, 2, 3)}
        xn_made = {n: sem(f"xn_made{n}") for n in (1, 2, 3)}
        x1T_ready, x1T_made = sem("x1T_ready"), sem("x1T_made")
        kexp_made, v2_made = sem("kexp_made"), sem("v2_made")
        score_ready, max_made, shifted = sem("score_ready"), sem("max_made"), sem("shifted")
        exp_made, pT_ready, pT_made, pv_ready = sem("exp_made"), sem("pT_ready"), sem("pT_made"), sem("pv_ready")
        rden_made, rdenm_made, attn_made = sem("rden_made"), sem("rdenm_made"), sem("attn_made")
        maskq_made = sem("maskq_made")
        attnT_ready, attnT_made, wp_ready = sem("attnT_ready"), sem("attnT_made"), sem("wp_ready")
        x2T_ready, x2T_made = sem("x2T_ready"), sem("x2T_made")
        lg_ready, lg_made = sem("lg_ready"), sem("lg_made")
        top_made, topi_made, topf_made = sem("top_made"), sem("topi_made"), sem("topf_made")
        nabs_made, expl_made, ln1p_made = sem("nabs_made"), sem("expl_made"), sem("ln1p_made")
        route_step = sem("route_step")
        sp_made, act_made, cf_made = sem("sp_made"), sem("act_made"), sem("cf_made")
        cfT_ready, cfT_made = sem("cfT_ready"), sem("cfT_made")
        cb_ready, hid_ready, silu_made, hw_made = sem("cb_ready"), sem("hid_ready"), sem("silu_made"), sem("hw_made")
        y_ready = sem("y_ready")

        w_in_act = sem("w_in_act")
        kb_made = sem("kb_made")
        pick_step = sem("pick_step")
        split_step, b2_step, bp_step = sem("split_step"), sem("b2_step"), sem("bp_step")
        eps_col = sb("eps_col", [P, 1])

        PREP = ["x0", "vec", "mask", "wp", "rw", "bias"] + [f"x{g}" for g in range(1, GROUPS)] + \
               [f"c{g}" for g in range(GROUPS)]
        prep_at = lambda name: PREP.index(name) + 1
        prep_bank = lambda n: (SC, MX, TR, PV)[n % 4]
        PREP_BIAS, PREP_ALL = prep_at("bias"), len(PREP)
        PREP_X = [prep_at(f"x{g}") for g in range(GROUPS)]
        MIDDLE = prep_at("x2")
        EARLY = prep_at("vec")
        SMALL = 8
        DVE_CONSTS = 14
        ROUTE = 5
        PICK = 6
        SPLIT = 4

        seqs = lambda buf, ct: buf[:, ct, :].rearrange("p (s k) -> p s k", k=PAD)[:, :, 1:PAD]
        flat = lambda ap: ap.rearrange("p t d -> p (t d)")
        toks = lambda ap: ap.rearrange("p (s k) -> p s k", k=S)
        tile = lambda ap, t: ap[:, t * P:(t + 1) * P]

        def head_start(engine, *sems):
            for s in sems:
                engine.sem_inc(s, 1)

        def groups(body, drain, finish, engine):
            body(0, None, None)
            body(1, 0, None)
            with engine.Fori(2, GROUPS) as i:
                body(i, i - 1, i - 2)
            drain(GROUPS - 1, GROUPS - 2)
            finish(GROUPS - 1)

        first = lambda g: isinstance(g, int) and g == 0

        second = lambda g: isinstance(g, int) and g == 1

        score_bank = lambda u, draining: (SC, ZV)[u % 2] if draining else SC
        hid_bank = lambda m, draining: (ZA, ZI, MX)[m % 3] if draining else (MX, CB)[m % 2]
        spread_bank = lambda m, draining: (ZA, ZI, CB)[m % 3] if draining else CB
        lg_bank = lambda draining: ZV if draining else CB

        block = stack.enter_context(nc.Block())

        @block.sync
        def _(sp):
            sp.sem_inc(out_done, 16)
            tok = lambda a: a.rearrange("(t b) s d -> (b s) t d", b=SEQ_T)
            row = lambda v: v.rearrange("(a n) -> a n", a=1)
            w3 = w_aiv.rearrange("d (p c) -> d p c", p=3)
            sp.dma_start(x_nat[:, 0:TG, :], tok(x)[:, 0:TG, :]).then_inc(x_in[0], 16)
            for n in range(4):
                cols = slice(n * REC // 4, (n + 1) * REC // 4)
                sp.dma_start(waiv_sb[:, :, cols], w3[:, :, cols]).then_inc(waiv_in[n], 16)
            for g in range(1, GROUPS):
                ts = slice(g * TG, (g + 1) * TG)
                sp.dma_start(x_nat[:, ts, :], tok(x)[:, ts, :]).then_inc(x_in[g], 16)
            for c in range(SEQ_T):
                sp.dma_start(mask_rows[:, c, :], mask).then_inc(small_in, 16)
            sp.wait_ge(dve_const, 2)
            sp.dma_start(mask_pair[:, :, :], mask.rearrange("(t b) s -> b t s", b=SEQ_T)).then_inc(small_in, 16)
            sp.dma_start(row_bias[0:1, 0:D], row(b_mix)).then_inc(small_in, 16)
            sp.dma_start(row_bias[0:1, D:], row(expert_bias)).then_inc(small_in, 16)
            sp.dma_start(bp_rows[:, :], row(bp).to_broadcast([ROWS, D])).then_inc(small_in, 16)
            sp.dma_start(wp_nat[:, :], wp).then_inc(small_in, 16)
            sp.dma_start(rw_nat[:, :], routing_w).then_inc(small_in, 16)
            for g in range(GROUPS):
                ts = slice(g * TG, (g + 1) * TG)
                sp.dma_start(ctx_nat[:, ts, :], tok(ctx_in)[:, ts, :]).then_inc(ctx_in_s[g], 16)
            sp.dma_start(wmix_sb[:, :, :], w_mix.rearrange("(c p) d -> p c d", p=P)).then_inc(w_in_act, 16)
            for half in range(2):
                sp.dma_start(ctx_key[half * S:(half + 1) * S, :, :],
                             ctx_in.rearrange("b s d -> s b d")).then_inc(key_in, 16)
            sp.dma_start(w1_sb[:, 0:E * HID].rearrange("d (e h) -> d e h", e=E),
                         r_w1.rearrange("e d h -> d e h")).then_inc(w_in, 16)
            sp.dma_start(w1_sb[:, E * HID:], s_w1).then_inc(w_in, 16)
            sp.dma_start(w2_sb[:, 0:MT, :], r_w2.rearrange("(m e) h d -> (e h) m d", e=2)).then_inc(w_in, 16)
            sp.dma_start(w2_sb[0:HID, MT, :], s_w2).then_inc(w_in, 16)
            nine = PART * PART
            sp.dma_start(b2_rows[0:E * nine, :], r_b2[:, None, :].to_broadcast([E, nine, D])).then_inc(w_in, 16)
            sp.dma_start(b2_rows[E * nine:, :], s_b2.rearrange("(a d) -> a d", a=1).to_broadcast([nine, D])).then_inc(w_in, 16)

            out_t = out.rearrange("(t b) s d -> (b s) t d", b=SEQ_T)

            with sp.Fori(0, GROUPS) as g:
                sp.wait_ge(xn_made[3], g * TG + TG + 1)
                sp.dma_start(out_t[:, bass.ds(g * TG, TG), :], y_out[:, :, :]).then_inc(out_done, 16)
            sp.wait_ge(out_done, 16 * GROUPS + 16)

        @block.gpsimd
        def _(pool):
            head_start(pool, v2_made)
            steps = [0]

            def step(ins):
                steps[0] += 1
                ins.then_inc(pool_step, 1)
                pool.wait_ge(pool_step, steps[0])

            step(nc.gpsimd.memset(ident[:, :], 0.0))
            nc.gpsimd.affine_select(out=ident[:, :], in_=ident[:, :], compare_op=ALU.not_equal, fill=1.0, base=0,
                                    pattern=[[-1, P]], channel_multiplier=1).then_inc(ident_made, 1)
            for half in range(2):
                km = kmask[half * S:(half + 1) * S, :]
                step(nc.gpsimd.memset(km, float(DK) ** -0.5))
                step(nc.gpsimd.affine_select(out=km, in_=km, compare_op=ALU.is_ge, fill=0.0, base=0,
                                             pattern=[[-DK, HH]], channel_multiplier=1))
                step(nc.gpsimd.affine_select(out=km, in_=km, compare_op=ALU.is_ge, fill=0.0, base=DK - 1,
                                             pattern=[[DK, HH]], channel_multiplier=-1))
            step(nc.gpsimd.memset(sel[:, :, :], 0.0))
            for i in range(PART):
                last = nc.gpsimd.affine_select(out=sel[:, :, :].rearrange("e m (b h) -> e m b h", b=2),
                                               in_=sel[:, :, :].rearrange("e m (b h) -> e m b h", b=2),
                                               compare_op=ALU.not_equal, fill=1.0, base=-PART * i,
                                               pattern=[[-2 * PART * PART, MT], [-PART * PART, 2], [0, HID]],
                                               channel_multiplier=1)
                if i < PART - 1:
                    step(last)
            last.then_inc(const_made, 1)
            step(nc.gpsimd.memset(part_one[:, :, :], 0.0))
            nc.gpsimd.affine_select(out=part_one[:, :, :], in_=part_one[:, :, :], compare_op=ALU.not_equal, fill=1.0,
                                    base=0, pattern=[[-1, PART], [-PART, ROWS // PART]],
                                    channel_multiplier=1).then_inc(const_made, 1)
            step(nc.gpsimd.memset(ind[:, :], 0.0))
            nc.gpsimd.affine_select(out=ind[:, :].rearrange("b (c q) -> b c q", c=SEQ_T),
                                    in_=ind[:, :].rearrange("b (c q) -> b c q", c=SEQ_T),
                                    compare_op=ALU.not_equal, fill=1.0, base=0,
                                    pattern=[[-1, SEQ_T], [0, S]], channel_multiplier=1).then_inc(const_made, 1)
            nc.gpsimd.iota(iota_i[:, :], pattern=[[0, TG], [1, E]], base=0, channel_multiplier=0).then_inc(const_made, 1)
            for n in range(TG):
                step(nc.gpsimd.memset(v2[n][:, :, :, :], 0.0))
                step(nc.gpsimd.memset(v2[n][0:S, :, :, DK:VC], 1.0))
                step(nc.gpsimd.memset(v2[n][S:P, :, :, VC + DK:2 * VC], 1.0))
            def square(g, ct):
                pool.wait_ge(a_clamped, g * CT + ct + 1)
                if not first(g):
                    pool.wait_ge(h_made, (g - 1) * CT + ct + 1)
                nc.gpsimd.tensor_tensor(seqs(q_buf, ct), seqs(a_buf, ct), seqs(a_buf, ct), ALU.mult).then_inc(a2_made, 1)

            def norm3(g):
                pool.wait_ge(rstd_made[3], g + 2)
                pool.nop(nofuse=True)
                mv, rs = norm_sb[3][1], norm_sb[3][3]
                for t in range(TG):
                    nc.gpsimd.tensor_scalar(r3[:, t, :], r3[:, t, :], mv[:, t, 0:1], rs[:, t:t + 1],
                                            ALU.subtract, ALU.mult).then_inc(xn_made[3], 1)

            def keys(g, t):
                if not (first(g) and t < 2):
                    pool.wait_ge(score_ready, g * UNITS + 2 * (t - 1) + 1)
                nc.gpsimd.tensor_tensor(kexp[t % 2][:, :, :],
                                        cT[:, bass.ds(g * TG + t, 1), :].to_broadcast([P, HH, P]),
                                        kmask[:, :, None].to_broadcast([P, HH, P]), ALU.mult).then_inc(kexp_made, 1)

            def values2(g, t):
                if not first(g):
                    pool.wait_ge(pv_ready, (g - 1) * UNITS + 2 * t + 2 + 1)
                pool.wait_ge(kexp_made, g * TG + t + 1)
                for half in range(2):
                    rows = slice(half * S, (half + 1) * S)
                    seq = bass.ds((g * TG + t) * SEQ_T, SEQ_T)
                    src = ctx_key[rows, seq, :].rearrange("k b (n h d) -> k b n h d", h=2, d=DK)[:, :, :, half, :]
                    nc.gpsimd.tensor_tensor(v2[t][rows, :, :, half * VC:half * VC + DK], src,
                                            mask_key[rows, seq][:, :, None, None].to_broadcast([S, SEQ_T, HH, DK]),
                                            ALU.mult).then_inc(v2_made, 1)
                    pool.wait_ge(v2_made, 2 * (g * TG + t) + half + 1 + 1)
            def iteration(gA, gB, gC):
                A, Bs = gA is not None, gB is not None
                for q in range(TG):
                    if A:
                        square(gA, 2 * q)
                        square(gA, 2 * q + 1)
                    if Bs and q < 2:
                        keys(gB, q + 2)
                        values2(gB, q + 2)
                if first(gA):
                    for g in range(GROUPS):
                        pool.wait_ge(prep_copied, PREP_BIAS)
                        pool.wait_ge(prep_copied, PREP_X[g])
                        xg = x_nat[:, g * TG:(g + 1) * TG, :]
                        nc.gpsimd.tensor_tensor(xg, xg, bias_bc[:, None, 0:D].to_broadcast([P, TG, D]),
                                                ALU.add).then_inc(xb_made, 1)
                    pool.wait_ge(prep_copied, PREP_ALL)
                    pool.wait_ge(key_in, 32)
                if A:
                    for t in range(2):
                        keys(gA, t)
                        values2(gA, t)
                if gC is not None:
                    norm3(gC)

            def drain(gB, gC):
                for t in (2, 3):
                    keys(gB, t)
                    values2(gB, t)
                norm3(gC)

            groups(iteration, drain, norm3, pool)

        @block.tensor
        def _(pe):
            def prep(n):
                name, to = PREP[n], prep_bank(n)
                if n >= 4:
                    pe.wait_ge(prep_copied, n - 3)
                if n == EARLY:
                    pe.wait_ge(small_in, 16 * SMALL)
                if name == "vec":
                    pe.wait_ge(vec_in, 16 * 4)
                    pe.wait_ge(dve_const, 1)
                    last = nc.tensor.transpose(to[:, 0:NV], vec_rows[:, :], ident[0:NV, 0:NV])
                elif name == "mask":
                    last = nc.tensor.transpose(to[:, 0:B], mask_rows[:, :, :].rearrange("b c s -> b (c s)"), ident[0:B, 0:B])
                elif name == "wp":
                    last = nc.tensor.transpose(to[:, 0:D], wp_nat[:, :], ident[:, :])
                elif name == "rw":
                    last = nc.tensor.transpose(to[:, 0:E], rw_nat[:, :], ident[0:E, 0:E])
                elif name == "bias":
                    pe.wait_ge(dve_const, 6)
                    last = nc.tensor.matmul(to[:, 0:D + E], ones_row[:, :], row_bias[:, :], start=True, stop=True)
                else:
                    src, came = (x_nat, x_in) if name[0] == "x" else (ctx_nat, ctx_in_s)
                    g = int(name[1:])
                    pe.wait_ge(came[g], 16)
                    for t in range(TG):
                        last = nc.tensor.transpose(tile(to, t), src[:, g * TG + t, :], ident[:, :])
                last.then_inc(prep_tr, 1)

            def project(g, ct):
                if first(g):
                    pe.wait_ge(waiv_in[ct // 2], 16)
                for p, (z, ready) in enumerate(((ZA, za_ready), (ZI, zi_ready), (ZV, zv_ready))):
                    if not (first(g) and ct == 0):
                        pe.wait_ge((a_made, i_made, iv_made)[p], g * CT + ct)
                    nc.tensor.matmul(z[:, :], waiv_sb[:, p, ct * P:(ct + 1) * P], xT[:, bass.ds(g * TOK, TOK)],
                                     start=True, stop=True).then_inc(ready, 1)

            def mix(gA, gC, ct):
                if ct == 0:
                    if first(gA):
                        pe.wait_ge(w_in_act, 16)
                    else:
                        pe.wait_ge(res_made[1], gA)
                    if gC is not None:
                        pe.wait_ge(hw_made, gC * MT + MT + 1)
                pe.wait_ge(h_made, gA * CT + ct + 1)
                states = h_buf[:, ct, :].rearrange("p (s k) -> p s k", k=PAD)[:, :, 1:PAD]
                last = nc.tensor.matmul(CB[:, :], wmix_sb[:, ct, :], states, start=(ct == 0), stop=(ct == CT - 1))
                if ct == CT - 1:
                    last.then_inc(mix_ready, 1)

            def turn_mix(g):
                pe.wait_ge(mixT_made, g + 1)
                for t in range(TG):
                    last = nc.tensor.transpose(tile(CB, t), tile(mixT, t), ident[:, :])
                last.then_inc(mix_turned, 1)

            def scores(g, u, draining=False):
                t, half = divmod(u, 2)
                if u == 0:
                    pe.wait_ge(x1T_made, g + 1)
                if half == 0:
                    pe.wait_ge(kexp_made, g * TG + t + 1)
                to = score_bank(u, draining)
                if draining and u == 1:
                    pe.wait_ge(lg_made, g)
                elif draining and u:
                    pe.wait_ge(shifted, g * UNITS + u - 1)
                elif u:
                    pe.wait_ge(shifted, g * UNITS + u)
                elif not first(g):
                    pe.wait_ge(res_made[2], g)
                pe.nop(nofuse=True)
                nc.tensor.matmul(to[:, :], ind[:, :],
                                 key_bias[:, bass.ds(g * TG + t, 1), :].to_broadcast([P, HH, S]),
                                 start=True, stop=False, skip_group_check=True)
                rows = slice(half * S, (half + 1) * S)
                for b in range(SEQ_T):
                    last = nc.tensor.matmul(to[b * S:(b + 1) * S, :], x1T[rows, t * P + b * S:t * P + (b + 1) * S],
                                            kexp[t % 2][rows, :, b * S:(b + 1) * S],
                                            start=False, stop=True, skip_group_check=True)
                last.then_inc(score_ready, 1)

            def turn_probs(g, u):
                pe.wait_ge(exp_made, g * UNITS + u + 1)
                pe.wait_ge(pT_made, g * UNITS + u + 1)
                for p in range(PAIRS):
                    last = nc.tensor.transpose(tile(TR, p), tile(prob[u % PB], p), ident[:, :])
                last.then_inc(pT_ready, 1)

            def values(g, u):
                t, half = divmod(u, 2)
                pe.wait_ge(pT_made, g * UNITS + u + 1 + 1)
                if half == 0:
                    pe.wait_ge(v2_made, 2 * (g * TG + t + 1) + 1)
                    pe.wait_ge(attn_made, g * TG + t + 1)
                for p in range(PAIRS):
                    pair = half * PAIRS + p
                    for b in range(SEQ_T):
                        last = nc.tensor.matmul(PV[b * S:(b + 1) * S, pair * 2 * VC:(pair + 1) * 2 * VC],
                                                probT[u % 2][:, p * P + b * S:p * P + (b + 1) * S],
                                                v2[t][:, b, pair, :], start=True, stop=True)
                last.then_inc(pv_ready, 1)

            def turn(to, src, made, g):
                for t in range(TG):
                    pe.wait_ge(made, g * TG + t + 1 + 1)
                    last = nc.tensor.transpose(tile(to, t), src[:, t, :], ident[:, :])
                return last

            def turn_attn(g):
                pe.wait_ge(pT_made, g * UNITS + UNITS + 1)
                turn(TR, attn, attn_made, g).then_inc(attnT_ready, 1)

            def out_proj(g):
                pe.wait_ge(shifted, g * UNITS + UNITS)
                nc.tensor.matmul(SC[:, :], three[:, :], bp_bf[:, None, :].to_broadcast([ROWS, TG, D]),
                                 start=True, stop=False, skip_group_check=True)
                pe.wait_ge(attnT_made, g + 1)
                for t in range(TG):
                    last = nc.tensor.matmul(tile(SC, t), tile(attnT, t), wpT[:, :], start=False, stop=True,
                                            skip_group_check=True)
                last.then_inc(wp_ready, 1)

            def turn_x2(g):
                pe.wait_ge(res_made[3], g + 1)
                turn(MX, x2, xn_made[2], g).then_inc(x2T_ready, 1)

            def logits(g, draining=False):
                pe.wait_ge(x2T_made, g + 1)
                if draining:
                    pe.wait_ge(iv_made, GROUPS * CT)
                    pe.wait_ge(shifted, (g + 1) * UNITS)
                else:
                    pe.wait_ge(res_made[1], g + 2)
                for t in range(TG):
                    last = nc.tensor.matmul(lg_bank(draining)[:, t * E:(t + 1) * E], tile(x2T, t), rwT[:, :],
                                            start=True, stop=True)
                last.then_inc(lg_ready, 1)

            def hidden(g, m, draining=False):
                width = P if m < MT else HID
                if draining:
                    if m >= 3:
                        pe.wait_ge(silu_made, g * (MT + 1) + m - 2 + 1)
                    elif m < 2:
                        pe.wait_ge((a_made, i_made)[m], GROUPS * CT)
                        pe.wait_ge(hw_made, g * MT + 1)
                elif m == 1:
                    pe.wait_ge(lg_made, g + 1)
                elif m >= 2:
                    pe.wait_ge(silu_made, g * (MT + 1) + m - 1 + 1)
                nc.tensor.matmul(hid_bank(m, draining)[0:width, :], w1_sb[:, m * P:m * P + width], x2T[:, :],
                                 start=True, stop=True).then_inc(hid_ready, 1)

            def turn_cf(g, draining=False):
                pe.wait_ge(cf_made, g + 1)
                if draining:
                    pe.wait_ge(res_made[1], GROUPS)
                    pe.wait_ge(hw_made, g * MT + 1)
                else:
                    pe.wait_ge(silu_made, g * (MT + 1) + MT + 1)
                for t in range(TG):
                    last = nc.tensor.matmul(CB[0:ROWS, t * P:(t + 1) * P], cf_part[:, t, :], ident_bf[:, :],
                                            start=True, stop=True)
                last.then_inc(cfT_ready, 1)

            def spread_cf(g, m, draining=False):
                if m == 0:
                    pe.wait_ge(cfT_made, g + 1)
                if draining:
                    if m < 2:
                        pe.wait_ge(silu_made, g * (MT + 1) + m + 4 + 1)
                    elif m == 3:
                        pe.wait_ge(hw_made, g * MT + 1 + 1)
                elif m:
                    pe.wait_ge(hw_made, g * MT + m + 1)
                nc.tensor.matmul(spread_bank(m, draining)[:, :], sel[:, m, :], cfT[:, :],
                                 start=True, stop=True).then_inc(cb_ready, 1)

            def experts_out(g, part):
                if part < 2:
                    pe.wait_ge(silu_made, (g + 1) * (MT + 1) + 1)
                if part >= 2:
                    pe.wait_ge(hw_made, g * MT + part)
                for t in range(TG):
                    if part == 0:
                        lhsT, rhs = tile(cfT, t), b2_bf[:, :]
                    elif part == 1:
                        lhsT, rhs = tile(hs[0:HID, MT, :], t), w2_sb[0:HID, MT, :]
                    else:
                        lhsT, rhs = tile(hw[:, part - 2, :], t), w2_sb[:, part - 2, :]
                    last = nc.tensor.matmul(tile(MX, t), lhsT, rhs, start=(part == 0 and t == 0),
                                            stop=(part == MT + 1), skip_group_check=True)
                if part == MT + 1:
                    last.then_inc(y_ready, 1)

            def turn_x1(g):
                if first(g):
                    pe.wait_ge(prep_copied, PREP_ALL)
                else:
                    pe.wait_ge(attnT_made, g)
                turn(TR, x1, xn_made[1], g).then_inc(x1T_ready, 1)

            def iteration(gA, gB, gC):
                A, Bs, C = gA is not None, gB is not None, gC is not None
                if A:
                    project(gA, 0)
                if Bs:
                    mix(gB, None, 7)
                if A:
                    project(gA, 1)
                if Bs:
                    turn_mix(gB)
                if C:
                    turn_x2(gC)
                    logits(gC)
                    hidden(gC, 0)
                if Bs:
                    turn_x1(gB)
                if A:
                    project(gA, 2)
                if Bs:
                    scores(gB, 0)
                if A:
                    project(gA, 3)
                if Bs:
                    scores(gB, 1)
                if first(gA):
                    for n in range(EARLY, MIDDLE):
                        prep(n)
                if A:
                    project(gA, 4)
                if Bs:
                    scores(gB, 2)
                if C:
                    hidden(gC, 1)
                if Bs:
                    scores(gB, 3)
                if A:
                    project(gA, 5)
                if Bs:
                    turn_probs(gB, 0)
                    scores(gB, 4)
                    values(gB, 0)
                    turn_probs(gB, 1)
                    scores(gB, 5)
                    values(gB, 1)
                    turn_probs(gB, 2)
                if A:
                    project(gA, 6)
                if Bs:
                    scores(gB, 6)
                    turn_probs(gB, 3)
                if A:
                    project(gA, 7)
                if Bs:
                    values(gB, 2)
                    values(gB, 3)
                if C:
                    hidden(gC, 2)
                    hidden(gC, 3)
                if Bs:
                    scores(gB, 7)
                if C:
                    hidden(gC, 4)
                if first(gA):
                    for n in range(MIDDLE, len(PREP)):
                        prep(n)
                    pe.wait_ge(const_made, 4)
                    pe.wait_ge(kb_made, 4)
                    pe.wait_ge(dve_const, DVE_CONSTS)
                    pe.wait_ge(bp_step, 2 * PART - 1 + PART)
                if C:
                    turn_cf(gC)
                    spread_cf(gC, 0)
                    experts_out(gC, 0)
                    experts_out(gC, 1)
                if Bs:
                    turn_probs(gB, 4)
                if C:
                    spread_cf(gC, 1)
                if Bs:
                    turn_probs(gB, 5)
                    values(gB, 4)
                    turn_probs(gB, 6)
                    values(gB, 5)
                    turn_probs(gB, 7)
                if C:
                    spread_cf(gC, 2)
                    experts_out(gC, 2)
                if Bs:
                    values(gB, 6)
                    values(gB, 7)
                if C:
                    spread_cf(gC, 3)
                if Bs:
                    turn_attn(gB)
                if C:
                    experts_out(gC, 3)
                if A:
                    mix(gA, gC, 0)
                if C:
                    experts_out(gC, 4)
                if Bs:
                    out_proj(gB)
                if C:
                    experts_out(gC, 5)
                if A:
                    mix(gA, gC, 1)
                    mix(gA, gC, 2)
                    mix(gA, gC, 3)
                    mix(gA, gC, 4)
                    mix(gA, gC, 5)
                    mix(gA, gC, 6)
                if second(gA):
                    pe.wait_ge(w_in, 16 * 6)
                    pe.wait_ge(b2_step, 2 * PART - 1 + PART)

            def drain(gB, gC):
                turn_x2(gC)
                mix(gB, None, 7)
                logits(gC, draining=True)
                hidden(gC, 0, draining=True)
                hidden(gC, 1, draining=True)
                turn_mix(gB)
                hidden(gC, 2, draining=True)
                turn_x1(gB)
                hidden(gC, 3, draining=True)
                scores(gB, 0, draining=True)
                hidden(gC, 4, draining=True)
                scores(gB, 1, draining=True)
                scores(gB, 2, draining=True)
                scores(gB, 3, draining=True)
                scores(gB, 4, draining=True)
                turn_probs(gB, 0)
                turn_probs(gB, 1)
                values(gB, 0)
                scores(gB, 5, draining=True)
                turn_probs(gB, 2)
                turn_cf(gC, draining=True)
                values(gB, 1)
                spread_cf(gC, 0, draining=True)
                experts_out(gC, 0)
                experts_out(gC, 1)
                turn_probs(gB, 3)
                values(gB, 2)
                scores(gB, 6, draining=True)
                spread_cf(gC, 1, draining=True)
                values(gB, 3)
                experts_out(gC, 2)
                spread_cf(gC, 2, draining=True)
                scores(gB, 7, draining=True)
                experts_out(gC, 3)
                spread_cf(gC, 3, draining=True)
                turn_probs(gB, 4)
                values(gB, 4)
                turn_probs(gB, 5)
                experts_out(gC, 4)
                values(gB, 5)
                turn_probs(gB, 6)
                experts_out(gC, 5)
                turn_probs(gB, 7)
                values(gB, 6)
                values(gB, 7)
                turn_attn(gB)
                out_proj(gB)

            def finish(gC):
                turn_x2(gC)
                logits(gC, draining=True)
                hidden(gC, 0, draining=True)
                hidden(gC, 1, draining=True)
                hidden(gC, 2, draining=True)
                turn_cf(gC, draining=True)
                hidden(gC, 3, draining=True)
                hidden(gC, 4, draining=True)
                spread_cf(gC, 0, draining=True)
                spread_cf(gC, 1, draining=True)
                experts_out(gC, 0)
                spread_cf(gC, 2, draining=True)
                spread_cf(gC, 3, draining=True)
                experts_out(gC, 1)
                experts_out(gC, 2)
                experts_out(gC, 3)
                experts_out(gC, 4)
                experts_out(gC, 5)

            head_start(pe, score_ready, pT_ready, pv_ready, attnT_ready, x1T_ready)
            pe.wait_ge(ident_made, 1)
            for n in range(EARLY):
                prep(n)
            pe.wait_ge(prep_copied, EARLY)
            groups(iteration, drain, finish, pe)

        @block.scalar
        def _(act):
            head_start(act, silu_made, pT_made, dev_made[1], dev_made[2], dev_made[3])
            row = lambda v: v.rearrange("(a n) -> a n", a=1)
            act.wait_ge(dve_const, 1)
            act.dma_start(vec_rows[0:CT, :], decay_bias.rearrange("(c p) -> c p", p=P)).then_inc(vec_in, 16)
            act.dma_start(vec_rows[R_B1:R_B1 + MT, :], r_b1.rearrange("(m e) h -> m (e h)", e=2)).then_inc(vec_in, 16)
            act.dma_start(vec_rows[R_B1 + MT:R_B1 + MT + 1, 0:HID], row(s_b1)).then_inc(vec_in, 16)
            act.dma_start(vec_rows[R_MASK:NV, :], mask.rearrange("(t b) s -> t (b s)", b=SEQ_T)).then_inc(vec_in, 16)

            def prep_copy(n):
                name, src = PREP[n], prep_bank(n)
                dst = {"vec": vec[:, :], "mask": mask_key[:, :], "wp": wpT[:, :], "rw": rwT[:, :], "bias": bias_bc[:, :]}.get(name)
                if dst is None:
                    g = int(name[1:])
                    dst = xT[:, g * TOK:(g + 1) * TOK] if name[0] == "x" else flat(cT[:, g * TG:(g + 1) * TG, :])
                act.wait_ge(prep_tr, n + 1)
                nc.scalar.activation(dst, src[:, 0:dst.shape[1]], ACT.Copy).then_inc(prep_copied, 1)

            def gates(g, ct):
                act.wait_ge(za_ready, g * CT + ct + 1)
                if not first(g):
                    act.wait_ge(h_made, (g - 1) * CT + ct + 1)
                nc.scalar.activation(seqs(a_buf, ct), toks(ZA[:, :]), ACT.Sigmoid, bias=vec[:, ct:ct + 1]).then_inc(a_made, 1)
                act.wait_ge(zi_ready, g * CT + ct + 1)
                if not first(g):
                    act.wait_ge(sig_made, (g - 1) * CT + ct + 1)
                nc.scalar.activation(iv_buf[:, ct, :], ZI[:, :], ACT.Sigmoid).then_inc(i_made, 1)

            def gate_sqrt(g, ct):
                act.wait_ge(a2_made, g * CT + ct + 1)
                nc.scalar.activation(seqs(q_buf, ct), seqs(q_buf, ct), ACT.Sqrt, bias=1.0, scale=-1.0).then_inc(s_made, 1)

            def exps(g, u):
                act.wait_ge(shifted, g * UNITS + u + 1)
                nc.scalar.activation(prob[u % PB][:, :], prob[u % PB][:, :], ACT.Exp).then_inc(exp_made, 1)

            def probs_turned(g, u):
                act.wait_ge(pT_ready, g * UNITS + u + 1 + 1)
                act.wait_ge(pv_ready, g * UNITS + max(0, u - 1) + 1)
                nc.scalar.activation(probT[u % 2][:, :], TR[:, :], ACT.Copy).then_inc(pT_made, 1)

            def deviation(n, g):
                act.wait_ge(mv_made[n], g * TG + TG)
                act.wait_ge(rstd_made[n], g + 1)
                nc.scalar.activation(norm_sb[n][2][:, :], norm_sb[n][1][:, :, 1], ACT.Sqrt,
                                     bias=eps_col[:, :]).then_inc(dev_made[n], 1)

            def mix_copied(g):
                act.wait_ge(mix_ready, g + 1)
                act.wait_ge(score_ready, g * UNITS + 1)
                nc.scalar.activation(mixT[:, :], CB[:, :], ACT.Copy).then_inc(mixT_made, 1)

            def x1_copied(g):
                act.wait_ge(x1T_ready, g + 2)
                nc.scalar.activation(x1T[:, :], TR[:, :], ACT.Copy).then_inc(x1T_made, 1)

            def attn_copied(g):
                act.wait_ge(attnT_ready, g + 2)
                nc.scalar.activation(attnT[:, :], TR[:, :], ACT.Copy).then_inc(attnT_made, 1)

            def x2_copied(g):
                act.wait_ge(x2T_ready, g + 1)
                nc.scalar.activation(x2T[:, :], MX[:, :], ACT.Copy).then_inc(x2T_made, 1)

            def route_exp(g):
                act.wait_ge(nabs_made, g + 1)
                nc.scalar.activation(rt[1][:, :, :], rt[0][:, :, :], ACT.Exp).then_inc(expl_made, 1)

            def route_ln(g):
                act.wait_ge(route_step, g * ROUTE + 1)
                nc.scalar.activation(rt[3][:, :, :], rt[2][:, :, :], ACT.Ln).then_inc(ln1p_made, 1)

            def route_sqrt(g):
                act.wait_ge(sp_made, g + 1)
                nc.scalar.activation(rt[9][:, :, :], rt[8][:, :, :], ACT.Sqrt).then_inc(act_made, 1)

            def combine_copied(g):
                act.wait_ge(cfT_ready, g + 1)
                nc.scalar.activation(cfT[:, :], CB[0:ROWS, :], ACT.Copy).then_inc(cfT_made, 1)

            def iteration(gA, gB, gC):
                A, Bs, C = gA is not None, gB is not None, gC is not None
                if A:
                    gates(gA, 0)
                if Bs:
                    mix_copied(gB)
                if C:
                    x2_copied(gC)
                if Bs:
                    deviation(1, gB)
                if A:
                    gates(gA, 1)
                if Bs:
                    x1_copied(gB)
                if A:
                    gates(gA, 2)
                    gates(gA, 3)
                if first(gA):
                    for n in range(EARLY, MIDDLE):
                        prep_copy(n)
                if A:
                    gates(gA, 4)
                if Bs:
                    nc.scalar.preload_act_table_set("natural_log_exp_and_others")
                    exps(gB, 0)
                if C:
                    nc.scalar.preload_act_table_set("natural_log_exp_and_others")
                if Bs:
                    exps(gB, 1)
                if C:
                    route_exp(gC)
                if Bs:
                    exps(gB, 2)
                    exps(gB, 3)
                if C:
                    route_ln(gC)
                if Bs:
                    probs_turned(gB, 0)
                if A:
                    gate_sqrt(gA, 0)
                if Bs:
                    probs_turned(gB, 1)
                if C:
                    route_sqrt(gC)
                if A:
                    gate_sqrt(gA, 1)
                    gate_sqrt(gA, 2)
                    gate_sqrt(gA, 3)
                    gates(gA, 5)
                    gates(gA, 6)
                if Bs:
                    probs_turned(gB, 2)
                    probs_turned(gB, 3)
                if A:
                    gates(gA, 7)
                if C:
                    silu(gC, 0)
                if first(gA):
                    for n in range(MIDDLE, len(PREP)):
                        prep_copy(n)
                if C:
                    silu(gC, 1)
                    silu(gC, 2)
                    silu(gC, 3)
                    silu(gC, 4)
                    combine_copied(gC)
                if Bs:
                    nc.scalar.preload_act_table_set("natural_log_exp_and_others")
                    exps(gB, 4)
                    exps(gB, 5)
                    exps(gB, 6)
                    exps(gB, 7)
                    probs_turned(gB, 4)
                if A:
                    gate_sqrt(gA, 4)
                if Bs:
                    probs_turned(gB, 5)
                    probs_turned(gB, 6)
                    probs_turned(gB, 7)
                if A:
                    gate_sqrt(gA, 5)
                    gate_sqrt(gA, 6)
                    gate_sqrt(gA, 7)
                if Bs:
                    attn_copied(gB)
                    deviation(2, gB)
                if C:
                    deviation(3, gC)

            def drain(gB, gC):
                x2_copied(gC)
                silu(gC, 0, draining=True)
                mix_copied(gB)
                deviation(1, gB)
                x1_copied(gB)
                silu(gC, 1, draining=True)
                silu(gC, 2, draining=True)
                silu(gC, 3, draining=True)
                silu(gC, 4, draining=True)
                route_exp(gC)
                nc.scalar.preload_act_table_set("natural_log_exp_and_others")
                route_ln(gC)
                exps(gB, 0)
                exps(gB, 1)
                exps(gB, 2)
                exps(gB, 3)
                probs_turned(gB, 0)
                probs_turned(gB, 1)
                route_sqrt(gC)
                combine_copied(gC)
                probs_turned(gB, 2)
                exps(gB, 4)
                probs_turned(gB, 3)
                nc.scalar.preload_act_table_set("natural_log_exp_and_others")
                exps(gB, 5)
                exps(gB, 6)
                exps(gB, 7)
                probs_turned(gB, 4)
                probs_turned(gB, 5)
                probs_turned(gB, 6)
                probs_turned(gB, 7)
                attn_copied(gB)
                deviation(2, gB)
                deviation(3, gC)

            def finish(gC):
                nc.scalar.preload_act_table_set("natural_log_exp_and_others")
                x2_copied(gC)
                route_exp(gC)
                route_ln(gC)
                route_sqrt(gC)
                silu(gC, 0, draining=True)
                silu(gC, 1, draining=True)
                silu(gC, 2, draining=True)
                combine_copied(gC)
                silu(gC, 3, draining=True)
                silu(gC, 4, draining=True)
                deviation(3, gC)

            def silu(g, m, draining=False):
                width = P if m < MT else HID
                act.wait_ge(hid_ready, g * (MT + 1) + m + 1)
                nc.scalar.activation(hs[0:width, m, :], hid_bank(m, draining)[0:width, :], ACT.Silu,
                                     bias=vec[0:width, R_B1 + m:R_B1 + m + 1]).then_inc(silu_made, 1)

            for n in range(EARLY):
                prep_copy(n)
            act.wait_ge(prep_copied, EARLY)
            groups(iteration, drain, finish, act)

        @block.vector
        def _(dve):
            head_start(dve, attn_made, hw_made, res_made[3], rstd_made[1], rstd_made[2], rstd_made[3], xn_made[1], xn_made[2], xn_made[3])
            nc.vector.memset(vec_rows[:, :], 0.0).then_inc(dve_const, 1)
            nc.vector.memset(row_bias[:, :], 0.0).then_inc(dve_const, 1)
            nc.vector.memset(ones_row[:, :], 0.0).then_inc(dve_const, 1)
            nc.vector.memset(cf_part[:, :, :], 0.0).then_inc(dve_const, 1)
            nc.vector.memset(key_bias[:, :, :], 0.0).then_inc(dve_const, 1)
            dve.wait_ge(dve_const, 3)
            nc.vector.memset(ones_row[0:1, :], 1.0).then_inc(dve_const, 1)
            dve.wait_ge(dve_const, 4)
            nc.vector.memset(cf_part[:, :, E * PART * PART:E * PART * PART + PART], 1.0).then_inc(dve_const, 1)
            nc.vector.memset(eps_col[:, :], EPS).then_inc(dve_const, 1)
            nc.vector.memset(three[:, :], 0.0).then_inc(dve_const, 1)
            dve.wait_ge(dve_const, 9)
            nc.vector.memset(three[0:PART, :], 1.0).then_inc(dve_const, 1)
            pads = lambda buf: buf.rearrange("p (s k) -> p s k", k=PAD)[:, :, 0]
            nc.vector.memset(restart[:, :], 0.0).then_inc(dve_const, 1)
            nc.vector.memset(a_buf[:, :, :].rearrange("p c (s k) -> p (c s) k", k=PAD)[:, :, 0], 0.0).then_inc(dve_const, 1)
            nc.vector.memset(q_buf[:, :, :].rearrange("p c (s k) -> p (c s) k", k=PAD)[:, :, 0], 0.0).then_inc(dve_const, 1)
            dve.wait_ge(dve_const, 11)
            nc.vector.memset(pads(restart[:, :]), GSTART).then_inc(dve_const, 1)
            dve.wait_ge(dve_const, DVE_CONSTS)
            steps = {"bp": 0, "b2": 0}

            def split(rows, to, name, done):
                def step(ins):
                    steps[name] += 1
                    ins.then_inc(done, 1)
                    dve.wait_ge(done, steps[name])

                for n in range(PART):
                    step(nc.vector.tensor_copy(b2_part[n][:, :], rows[:, :]))
                    if n < PART - 1:
                        step(nc.vector.tensor_tensor(rows[:, :], rows[:, :], b2_part[n][:, :], ALU.subtract))
                step(nc.vector.tensor_scalar(to[:, :], b2_part[0][:, :], part_of[:, 0:1], None, ALU.mult))
                for n in range(1, PART):
                    step(nc.vector.scalar_tensor_tensor(to[:, :], b2_part[n][:, :], part_of[:, n:n + 1], to[:, :],
                                                        ALU.mult, ALU.add))

            def stage_b_constants():
                dve.wait_ge(small_in, 16 * SMALL)
                nc.vector.tensor_scalar(key_bias[0:SEQ_T, :, :], mask_pair[:, :, :], 0.0, NEG, ALU.is_equal, ALU.mult).then_inc(kb_made, 1)
                dve.wait_ge(const_made, 4)
                nc.vector.tensor_copy(flat(iota_f[:, :, :]), iota_i[:, :]).then_inc(kb_made, 1)
                nc.vector.tensor_reduce(part_of[:, :], part_one[:, :, :], AXX, ALU.add).then_inc(kb_made, 1)
                dve.wait_ge(ident_made, 1)
                nc.vector.tensor_copy(ident_bf[:, :], ident[:, :]).then_inc(kb_made, 1)
                dve.wait_ge(kb_made, 4)
                split(bp_rows, bp_bf, "bp", bp_step)

            def split_b2():
                dve.wait_ge(w_in, 16 * 6)
                split(b2_rows, b2_bf, "b2", b2_step)

            def clamp_gate(g, ct):
                dve.wait_ge(a_made, g * CT + ct + 1)
                nc.vector.tensor_scalar(seqs(a_buf, ct), seqs(a_buf, ct), TINY, 1.0, ALU.max, ALU.min).then_inc(a_clamped, 1)
                dve.wait_ge(i_made, g * CT + ct + 1)
                dve.wait_ge(zv_ready, g * CT + ct + 1)
                nc.vector.tensor_tensor(iv_buf[:, ct, :], ZV[:, :], iv_buf[:, ct, :], ALU.mult).then_inc(iv_made, 1)

            def scan_decay(g, ct):
                dve.wait_ge(a_clamped, g * CT + ct + 1)
                if not first(g) and ct == 0:
                    dve.wait_ge(mix_ready, g)
                nc.vector.tensor_tensor_scan(h_buf[:, ct, :], a_buf[:, ct, :], restart[:, :], 0.0,
                                             ALU.mult, ALU.add).then_inc(g_made, 1)

            def scan_state(g, ct):
                at = g * CT + ct + 1
                dve.wait_ge(s_made, at)
                dve.wait_ge(iv_made, at)
                nc.vector.scalar_tensor_tensor(seqs(q_buf, ct), seqs(q_buf, ct), CLAMP, toks(iv_buf[:, ct, :]),
                                               ALU.max, ALU.mult).then_inc(sig_made, 1)
                dve.wait_ge(sig_made, at)
                dve.wait_ge(g_made, at)
                nc.vector.scalar_tensor_tensor(q_buf[:, ct, :], h_buf[:, ct, :], 1.0, q_buf[:, ct, :],
                                               ALU.min, ALU.mult).then_inc(u_made, 1)
                dve.wait_ge(u_made, at)
                nc.vector.tensor_tensor_scan(h_buf[:, ct, :], a_buf[:, ct, :], q_buf[:, ct, :], 0.0,
                                             ALU.mult, ALU.add).then_inc(h_made, 1)

            def shift(g, u, draining=False):
                s3 = lambda a: a.rearrange("p (h k) -> p h k", k=S)
                scored = score_bank(u, draining)
                dve.wait_ge(score_ready, g * UNITS + u + 1 + 1)
                nc.vector.tensor_reduce(smax[:, u % 2, :], s3(scored[:, :]), AXX, ALU.max).then_inc(max_made, 1)
                dve.wait_ge(max_made, g * UNITS + u + 1)
                dve.wait_ge(pT_ready, g * UNITS + max(0, u - PB + 1) + 1)
                nc.vector.tensor_tensor(s3(prob[u % PB][:, :]), s3(scored[:, :]),
                                        smax[:, u % 2, :].unsqueeze(2).to_broadcast([P, HH, S]),
                                        ALU.subtract).then_inc(shifted, 1)

            def attend(g, t):
                pv = PV[:, 0:NH * VC].rearrange("p (h c) -> p h c", c=VC)
                dve.wait_ge(pv_ready, g * UNITS + 2 * t + 2 + 1)
                nc.vector.reciprocal(rden[:, t % 2, :], pv[:, :, DK]).then_inc(rden_made, 1)
                dve.wait_ge(rden_made, g * TG + t + 1)
                dve.wait_ge(maskq_made, g + 1)
                nc.vector.tensor_scalar(rdenm[:, t % 2, :], rden[:, t % 2, :], mask_q[:, t:t + 1], None,
                                        ALU.mult).then_inc(rdenm_made, 1)
                dve.wait_ge(rdenm_made, g * TG + t + 1)
                if t == 0:
                    dve.wait_ge(attnT_ready, g + 1)
                nc.vector.tensor_tensor(attn[:, t, :].rearrange("p (h c) -> p h c", c=DK), pv[:, :, 0:DK],
                                        rdenm[:, t % 2, :].unsqueeze(2).to_broadcast([P, NH, DK]),
                                        ALU.mult).then_inc(attn_made, 1)

            def stats(n, g, r):
                st, mv, ln, rs = norm_sb[n]
                dve.wait_ge(res_made[n], g + (2 if n == 3 else 1))
                for t in range(TG):
                    nc.vector.bn_stats(st[:, t, :], r[:, t, :]).then_inc(st_made[n], 1)
                dve.wait_ge(dev_made[n], g + 1)
                if n == 3:
                    dve.wait_ge(xn_made[3], g * TG + 1)
                for t in range(TG):
                    dve.wait_ge(st_made[n], g * TG + t + 1)
                    dve.nop(nofuse=True)
                    nc.vector.bn_aggr(mv[:, t, :], st[:, t, :]).then_inc(mv_made[n], 1)

            def inverse(n, g):
                st, mv, ln, rs = norm_sb[n]
                dve.wait_ge(dev_made[n], g + 2)
                if n == 3 and not first(g):
                    dve.wait_ge(xn_made[3], g * TG + 1)
                nc.vector.reciprocal(rs[:, :], ln[:, :]).then_inc(rstd_made[n], 1)

            def normalise(n, g, r, xn):
                st, mv, ln, rs = norm_sb[n]
                inverse(n, g)
                dve.wait_ge(rstd_made[n], g + 2)
                for t in range(TG):
                    nc.vector.tensor_scalar(xn[:, t, :], r[:, t, :], mv[:, t, 0:1], rs[:, t:t + 1],
                                            ALU.subtract, ALU.mult).then_inc(xn_made[n], 1)

            def residual1(g):
                dve.wait_ge(mix_turned, g + 1)
                dve.wait_ge(x1T_ready, g + 1)
                dve.wait_ge(xb_made, g + 1)
                nc.vector.tensor_tensor(flat(r1[:, :, :]), CB[:, :],
                                        x_nat[:, bass.ds(g * TG, TG), :].rearrange("p t d -> p (t d)"),
                                        ALU.add).then_inc(res_made[1], 1)
                stats(1, g, r1)

            def norm1(g):
                normalise(1, g, r1, x1)

            def residual2(g):
                dve.wait_ge(wp_ready, g + 1)
                if not first(g):
                    dve.wait_ge(x2T_ready, g)
                for t in range(TG):
                    last = nc.vector.scalar_tensor_tensor(r2[:, t, :], tile(SC, t), mask_q[:, t:t + 1], x1[:, t, :],
                                                          ALU.mult, ALU.add)
                last.then_inc(res_made[2], 1)
                stats(2, g, r2)

            def route_logits(g, draining=False):
                dve.wait_ge(lg_ready, g + 1)
                nc.vector.tensor_tensor(lg[:, :, :], lg_bank(draining)[:, 0:TG * E].rearrange("p (t e) -> p t e", e=E),
                                        bias_bc[:, None, D:].to_broadcast([P, TG, E]), ALU.add).then_inc(lg_made, 1)
                dve.wait_ge(lg_made, g + 1)
                nc.vector.scalar_tensor_tensor(rt[0][:, :, :], lg[:, :, :], -1.0, lg[:, :, :], ALU.mult, ALU.min).then_inc(nabs_made, 1)
                for t in range(TG):
                    nc.vector.max(top[:, t, :], lg[:, t, :]).then_inc(top_made, 1)
                for t in range(TG):
                    dve.wait_ge(top_made, g * TG + t + 1)
                    dve.nop(nofuse=True)
                    nc.vector.max_index(top_i[:, t, :], top[:, t, :], lg[:, t, :]).then_inc(topi_made, 1)
                dve.wait_ge(topi_made, g * TG + TG)
                nc.vector.tensor_copy(top_f[:, :, :], top_i[:, :, :]).then_inc(topf_made, 1)

            e, u, dlt, dg, rc = rt[1], rt[2], rt[4], rt[5], rt[6]

            def route_log(g):
                step = lambda n: dve.wait_ge(route_step, g * ROUTE + n)
                dve.wait_ge(expl_made, g + 1)
                nc.vector.tensor_scalar(u[:, :, :], e[:, :, :], 1.0, None, ALU.add).then_inc(route_step, 1)
                step(1)
                nc.vector.tensor_scalar(dlt[:, :, :], u[:, :, :], 1.0, None, ALU.subtract).then_inc(route_step, 1)
                nc.vector.tensor_scalar(rt[11][:, :, :], u[:, :, :], 1.0, None, ALU.is_equal).then_inc(route_step, 1)
                step(2)
                nc.vector.tensor_scalar(dg[:, :, :], dlt[:, :, :], 1e-30, None, ALU.max).then_inc(route_step, 1)
                step(4)
                nc.vector.reciprocal(rc[:, :, :], dg[:, :, :]).then_inc(route_step, 1)
                dve.wait_ge(topf_made, g + 1)
                pick = lambda n: top_f[:, :, n:n + 1].to_broadcast([P, TG, E])
                nc.vector.tensor_tensor(rt[10][:, :, :], iota_f[:, :, :], pick(0), ALU.is_equal).then_inc(pick_step, 1)
                nc.vector.tensor_tensor(rt[7][:, :, :], iota_f[:, :, :], pick(1), ALU.is_equal).then_inc(pick_step, 1)
                dve.wait_ge(pick_step, g * PICK + 2)
                nc.vector.tensor_tensor(rt[10][:, :, :], rt[10][:, :, :], rt[7][:, :, :], ALU.add).then_inc(pick_step, 1)

            def route_softplus(g):
                dve.wait_ge(ln1p_made, g + 1)
                dve.wait_ge(route_step, g * ROUTE + 5)
                nc.vector.tensor_tensor(rt[3][:, :, :], rt[3][:, :, :], rc[:, :, :], ALU.mult).then_inc(pick_step, 1)
                dve.wait_ge(pick_step, g * PICK + 4)
                nc.vector.tensor_tensor(rt[3][:, :, :], rt[3][:, :, :], rt[11][:, :, :], ALU.add).then_inc(pick_step, 1)
                dve.wait_ge(pick_step, g * PICK + 5)
                nc.vector.tensor_tensor(rt[3][:, :, :], rt[3][:, :, :], e[:, :, :], ALU.mult).then_inc(pick_step, 1)
                dve.wait_ge(pick_step, g * PICK + 6)
                nc.vector.scalar_tensor_tensor(rt[8][:, :, :], lg[:, :, :], 0.0, rt[3][:, :, :], ALU.max, ALU.add).then_inc(sp_made, 1)

            def route_combine(g):
                dve.wait_ge(act_made, g + 1)
                split = lambda n: dve.wait_ge(split_step, g * SPLIT + n)
                part = cf_part[:, :, 0:E * PART * PART].rearrange("p t (e i j) -> p t e i j", i=PART, j=PART)
                over_j = lambda ap: ap.unsqueeze(3).to_broadcast([P, TG, E, PART])
                nc.vector.tensor_tensor(cf[:, :, :], rt[9][:, :, :], rt[10][:, :, :], ALU.mult).then_inc(split_step, 1)
                split(1)
                if not first(g):
                    dve.wait_ge(cfT_ready, g)
                nc.vector.tensor_copy(part[:, :, :, 0, :], over_j(cf[:, :, :])).then_inc(split_step, 1)
                split(2)
                nc.vector.tensor_tensor(cf_rest[:, :, :], cf[:, :, :], part[:, :, :, 0, 0], ALU.subtract).then_inc(split_step, 1)
                split(3)
                nc.vector.tensor_copy(part[:, :, :, 1, :], over_j(cf_rest[:, :, :])).then_inc(split_step, 1)
                split(4)
                nc.vector.tensor_tensor(part[:, :, :, 2, :], over_j(cf_rest[:, :, :]), part[:, :, :, 1, :],
                                        ALU.subtract).then_inc(cf_made, 1)

            def weigh(g, m, draining=False):
                dve.wait_ge(cb_ready, g * MT + m + 1)
                dve.wait_ge(silu_made, g * (MT + 1) + m + 1 + 1)
                nc.vector.tensor_tensor(hw[:, m, :], spread_bank(m, draining)[:, :], hs[:, m, :], ALU.mult).then_inc(hw_made, 1)

            def residual3(g):
                dve.wait_ge(y_ready, g + 1)
                dve.wait_ge(out_done, 16 * g + 16)
                nc.vector.tensor_tensor(flat(r3[:, :, :]), MX[:, :], flat(x2[:, :, :]), ALU.add).then_inc(res_made[3], 1)
                stats(3, g, r3)

            def query_mask(g):
                dve.wait_ge(prep_copied, PREP_ALL)
                nc.vector.tensor_copy(mask_q[:, :], vec[:, bass.ds(R_MASK + g * TG, TG)]).then_inc(maskq_made, 1)

            def iteration(gA, gB, gC):
                A, Bs, C = gA is not None, gB is not None, gC is not None
                if A:
                    clamp_gate(gA, 0)
                if C:
                    normalise(2, gC, r2, x2)
                if Bs:
                    residual1(gB)
                    norm1(gB)
                if A:
                    clamp_gate(gA, 1)
                if C:
                    route_logits(gC)
                if A:
                    clamp_gate(gA, 2)
                    scan_decay(gA, 0)
                    scan_decay(gA, 1)
                if Bs:
                    shift(gB, 0)
                if A:
                    scan_decay(gA, 2)
                if Bs:
                    query_mask(gB)
                if A:
                    clamp_gate(gA, 3)
                    scan_decay(gA, 3)
                if Bs:
                    shift(gB, 1)
                if first(gA):
                    stage_b_constants()
                if A:
                    clamp_gate(gA, 4)
                if Bs:
                    shift(gB, 2)
                    shift(gB, 3)
                if C:
                    route_log(gC)
                if A:
                    scan_decay(gA, 4)
                if C:
                    route_softplus(gC)
                if Bs:
                    shift(gB, 4)
                if A:
                    scan_state(gA, 0)
                if Bs:
                    shift(gB, 5)
                if A:
                    scan_state(gA, 1)
                    clamp_gate(gA, 5)
                if Bs:
                    attend(gB, 0)
                if A:
                    scan_decay(gA, 5)
                    clamp_gate(gA, 6)
                if C:
                    route_combine(gC)
                if Bs:
                    shift(gB, 6)
                    attend(gB, 1)
                if A:
                    scan_state(gA, 2)
                    scan_decay(gA, 6)
                if Bs:
                    shift(gB, 7)
                if A:
                    scan_state(gA, 3)
                    clamp_gate(gA, 7)
                    scan_decay(gA, 7)
                if C:
                    weigh(gC, 0)
                if A:
                    scan_state(gA, 4)
                if C:
                    weigh(gC, 1)
                    weigh(gC, 2)
                if Bs:
                    attend(gB, 2)
                if A:
                    scan_state(gA, 5)
                if Bs:
                    attend(gB, 3)
                if C:
                    weigh(gC, 3)
                if A:
                    scan_state(gA, 6)
                    scan_state(gA, 7)
                if Bs:
                    residual2(gB)
                if C:
                    residual3(gC)
                if second(gA):
                    split_b2()
                if C:
                    inverse(3, gC)

            def drain(gB, gC):
                normalise(2, gC, r2, x2)
                residual1(gB)
                norm1(gB)
                shift(gB, 0, draining=True)
                query_mask(gB)
                route_logits(gC, draining=True)
                shift(gB, 1, draining=True)
                route_log(gC)
                shift(gB, 2, draining=True)
                shift(gB, 3, draining=True)
                route_softplus(gC)
                route_combine(gC)
                shift(gB, 4, draining=True)
                attend(gB, 0)
                shift(gB, 5, draining=True)
                shift(gB, 6, draining=True)
                weigh(gC, 0, draining=True)
                weigh(gC, 1, draining=True)
                weigh(gC, 2, draining=True)
                shift(gB, 7, draining=True)
                weigh(gC, 3, draining=True)
                attend(gB, 1)
                attend(gB, 2)
                attend(gB, 3)
                residual3(gC)
                residual2(gB)
                inverse(3, gC)

            def finish(gC):
                normalise(2, gC, r2, x2)
                route_logits(gC, draining=True)
                route_log(gC)
                route_softplus(gC)
                route_combine(gC)
                weigh(gC, 0, draining=True)
                weigh(gC, 1, draining=True)
                weigh(gC, 2, draining=True)
                weigh(gC, 3, draining=True)
                residual3(gC)
                inverse(3, gC)

            groups(iteration, drain, finish, dve)


_INS = ['x', 'ctx_1024', 'mask_BxS2_fk1', 'L0_attn_W_aiv', 'L0_attn_decay_bias', 'L0_attn_W_mix',
        'L0_attn_b_mix', 'L0_xattn_Wp', 'L0_xattn_bp', 'L0_ffn_routing_W', 'L0_ffn_expert_bias',
        'L0_ffn_sW1', 'L0_ffn_sb1', 'L0_ffn_sW2', 'L0_ffn_sb2', 'L0_ffn_rW1', 'L0_ffn_rb1',
        'L0_ffn_rW2', 'L0_ffn_rb2']
_OUTS = [((32, 64, 128), 'float32')]


def kernel(**inputs):
    import numpy as _np
    import concourse.bacc as _bacc
    from concourse import mybir as _mybir
    from concourse.bass_utils import run_bass_kernel_spmd as _run

    nc = _bacc.Bacc("TRN2", target_bir_lowering=False, num_devices=1)
    arrays, args = {}, []
    for name in _INS:
        a = _np.ascontiguousarray(inputs[name])
        arrays[f"in_{name}_dram"] = a
        args.append(nc.dram_tensor(f"in_{name}_dram", a.shape, _mybir.dt.from_np(a.dtype), kind="ExternalInput").ap())
    for i, (shape, dtype) in enumerate(_OUTS):
        dt = _mybir.dt.from_np(_np.dtype(dtype))
        args.append(nc.dram_tensor(f"out_{i}_dram", shape, dt, kind="ExternalOutput").ap())
    decoder_layer(nc, *args)
    r = _run(nc, [arrays], core_ids=[0])
    return r.results[0]["out_0_dram"]
```
